# Optimizing a Trainium2 kernel written in Bass

```python
import numpy as np
import jax
import jax.numpy as jnp

def _softmax(x, axis=-1):
    return jax.nn.softmax(x, axis=axis)

def _gelu(x):
    return jax.nn.gelu(x, approximate=True)

def _silu(x):
    return jax.nn.silu(x)

def _sigmoid(x):
    return jax.nn.sigmoid(x)

def _layernorm(x, axis=-1, eps=1e-05):
    m = jnp.mean(x, axis=axis, keepdims=True)
    v = jnp.var(x, axis=axis, keepdims=True)
    return (x - m) / jnp.sqrt(v + eps)

def _scatter_add(tgt, idx, src, axis=0):
    return tgt.at[idx].add(src)

def _segment_sum(src, seg, n):
    return jax.ops.segment_sum(src, seg, n)
kernel_name = 'mk_metaformer_d2_conv_nhwc256_r4_9fd320'

def setup_inputs(seed: int=0):
    np.random.seed(seed)
    _w = jnp.asarray

    def _rec_inputs():
        import jax
        import jax.numpy as jnp
        _gk = jax.random.key(seed)
        x = -0.000125 + 0.9999 * jax.random.normal(jax.random.fold_in(_gk, 1), (32, 16, 16, 64), jnp.float32)
        return x
    x = _rec_inputs()

    def _L0_conv_setup():
        import jax, jax.numpy as jnp
        import numpy as np
        WS = 8
        HEADS = 8
        HEAD_DIM = 32
        DIM = 64
        DISP = WS // 2
        NEG = float('-inf')

        def _masks():
            n = WS * WS
            m = DISP * WS
            ul = np.zeros((n, n), np.float32)
            ul[-m:, :-m] = NEG
            ul[:-m, -m:] = NEG
            lr = np.zeros((WS, WS, WS, WS), np.float32)
            lr[:, -DISP:, :, :-DISP] = NEG
            lr[:, :-DISP, :, -DISP:] = NEG
            return (jnp.asarray(ul), jnp.asarray(lr.reshape(n, n)))

        def _rel_idx():
            idx = np.array([[x, y] for x in range(WS) for y in range(WS)])
            return idx[None, :, :] - idx[:, None, :] + WS - 1
        key = jax.random.key(seed)
        ks = jax.random.split(key, 5)
        b, H, W = (32, 16, 16)
        inner = HEADS * HEAD_DIM
        return {'x': jax.random.normal(ks[0], (b, H, W, DIM), jnp.float32), 'w_qkv': jax.random.normal(ks[1], (DIM, 3 * inner), jnp.float32) / np.sqrt(DIM).astype(np.float32), 'pos_emb': jax.random.normal(ks[2], (2 * WS - 1, 2 * WS - 1), jnp.float32), 'w_out': jax.random.normal(ks[3], (inner, DIM), jnp.float32) / np.sqrt(inner).astype(np.float32), 'b_out': jax.random.normal(ks[4], (DIM,), jnp.float32)}
    _L0_conv_all = _L0_conv_setup()
    _L0_conv_in = {k: v for k, v in _L0_conv_all.items() if k in ('w_qkv', 'pos_emb', 'w_out', 'b_out')}
    del _L0_conv_all

    def _L0_ffn_setup():
        import jax, jax.numpy as jnp
        import numpy as np
        D_MODEL = 64
        N_EXPERTS = 16
        HIDDEN = 128
        SCALE = 0.02
        key = jax.random.key(seed)
        ks = jax.random.split(key, 5)
        x = jax.random.normal(ks[0], (4, 2048, D_MODEL), dtype=jnp.float32)
        gate_w = jax.random.normal(ks[1], (D_MODEL, N_EXPERTS), dtype=jnp.float32) * SCALE
        gate_b = jnp.zeros((N_EXPERTS,), dtype=jnp.float32)
        w1 = jax.random.normal(ks[2], (N_EXPERTS, D_MODEL, HIDDEN), dtype=jnp.float32) * SCALE
        w2 = jax.random.normal(ks[3], (N_EXPERTS, D_MODEL, HIDDEN), dtype=jnp.float32) * SCALE
        w3 = jax.random.normal(ks[4], (N_EXPERTS, HIDDEN, D_MODEL), dtype=jnp.float32) * SCALE
        return {'x': x, 'gate_w': gate_w, 'gate_b': gate_b, 'w1': w1, 'w2': w2, 'w3': w3}
    _L0_ffn_all = _L0_ffn_setup()
    _L0_ffn_in = {k: v for k, v in _L0_ffn_all.items() if k in ('gate_w', 'gate_b', 'w1', 'w2', 'w3')}
    del _L0_ffn_all

    def _L1_conv_setup():
        import jax, jax.numpy as jnp
        import numpy as np
        B, H, W, C = (16, 16, 16, 64)
        key = jax.random.key(seed)
        ks = jax.random.split(key, 4)
        x = jax.random.normal(ks[0], (B, H, W, C), dtype=jnp.float32)
        w1 = jax.random.normal(ks[1], (C,), dtype=jnp.float32) * C ** (-0.5)
        w2 = jax.random.normal(ks[2], (C,), dtype=jnp.float32) * C ** (-0.5)
        w3 = jax.random.normal(ks[3], (C,), dtype=jnp.float32) * C ** (-0.5)
        b1 = jnp.zeros((1,), jnp.float32)
        b2 = jnp.zeros((1,), jnp.float32)
        b3 = jnp.zeros((1,), jnp.float32)
        return {'x': x, 'w1': w1, 'b1': b1, 'w2': w2, 'b2': b2, 'w3': w3, 'b3': b3}
    _L1_conv_all = _L1_conv_setup()
    _L1_conv_in = {k: v for k, v in _L1_conv_all.items() if k in ('w1', 'b1', 'w2', 'b2', 'w3', 'b3')}
    del _L1_conv_all

    def _L1_ffn_setup():
        import jax, jax.numpy as jnp
        import numpy as np
        N_EXPERTS = 8
        TOP_K = 2
        key = jax.random.key(seed)
        ks = jax.random.split(key, 5)
        B, T, C, E, H = (8, 512, 64, 8, 682)
        scale = 1.0 / np.sqrt(C)
        return {'x': jax.random.normal(ks[0], (B, T, C), dtype=jnp.float32), 'router_w': jax.random.normal(ks[1], (E, C), dtype=jnp.float32) * scale, 'w1': jax.random.normal(ks[2], (E, H, C), dtype=jnp.float32) * scale, 'w2': jax.random.normal(ks[3], (E, C, H), dtype=jnp.float32) * (1.0 / np.sqrt(H)), 'w3': jax.random.normal(ks[4], (E, H, C), dtype=jnp.float32) * scale}
    _L1_ffn_all = _L1_ffn_setup()
    _L1_ffn_in = {k: v for k, v in _L1_ffn_all.items() if k in ('router_w', 'w1', 'w2', 'w3')}
    del _L1_ffn_all
    return {'x': x, 'L0_conv_w_qkv': _L0_conv_in['w_qkv'], 'L0_conv_pos_emb': _L0_conv_in['pos_emb'], 'L0_conv_w_out': _L0_conv_in['w_out'], 'L0_conv_b_out': _L0_conv_in['b_out'], 'L0_ffn_gate_w': _L0_ffn_in['gate_w'], 'L0_ffn_gate_b': _L0_ffn_in['gate_b'], 'L0_ffn_w1': _L0_ffn_in['w1'], 'L0_ffn_w2': _L0_ffn_in['w2'], 'L0_ffn_w3': _L0_ffn_in['w3'], 'L1_conv_w1': _L1_conv_in['w1'], 'L1_conv_b1': _L1_conv_in['b1'], 'L1_conv_w2': _L1_conv_in['w2'], 'L1_conv_b2': _L1_conv_in['b2'], 'L1_conv_w3': _L1_conv_in['w3'], 'L1_conv_b3': _L1_conv_in['b3'], 'L1_ffn_router_w': _L1_ffn_in['router_w'], 'L1_ffn_w1': _L1_ffn_in['w1'], 'L1_ffn_w2': _L1_ffn_in['w2'], 'L1_ffn_w3': _L1_ffn_in['w3']}

def reference(x, L0_conv_w_qkv, L0_conv_pos_emb, L0_conv_w_out, L0_conv_b_out, L0_ffn_gate_w, L0_ffn_gate_b, L0_ffn_w1, L0_ffn_w2, L0_ffn_w3, L1_conv_w1, L1_conv_b1, L1_conv_w2, L1_conv_b2, L1_conv_w3, L1_conv_b3, L1_ffn_router_w, L1_ffn_w1, L1_ffn_w2, L1_ffn_w3):
    import jax
    import jax.numpy as jnp

    def _L0_conv_ref(x, w_qkv, pos_emb, w_out, b_out):
        import jax, jax.numpy as jnp
        import numpy as np
        WS = 8
        HEADS = 8
        HEAD_DIM = 32
        DIM = 64
        DISP = WS // 2
        NEG = float('-inf')

        def _masks():
            n = WS * WS
            m = DISP * WS
            ul = np.zeros((n, n), np.float32)
            ul[-m:, :-m] = NEG
            ul[:-m, -m:] = NEG
            lr = np.zeros((WS, WS, WS, WS), np.float32)
            lr[:, -DISP:, :, :-DISP] = NEG
            lr[:, :-DISP, :, -DISP:] = NEG
            return (jnp.asarray(ul), jnp.asarray(lr.reshape(n, n)))

        def _rel_idx():
            idx = np.array([[x, y] for x in range(WS) for y in range(WS)])
            return idx[None, :, :] - idx[:, None, :] + WS - 1
        b, H, W, _ = x.shape
        nWH, nWW = (H // WS, W // WS)
        scale = HEAD_DIM ** (-0.5)
        x = jnp.roll(x, (-DISP, -DISP), axis=(1, 2))
        qkv = x @ w_qkv

        def to_win(t):
            t = t.reshape(b, nWH, WS, nWW, WS, HEADS, HEAD_DIM)
            t = t.transpose(0, 5, 1, 3, 2, 4, 6)
            return t.reshape(b, HEADS, nWH * nWW, WS * WS, HEAD_DIM)
        q, k, v = map(to_win, jnp.split(qkv, 3, axis=-1))
        rel = _rel_idx()
        bias = pos_emb[rel[..., 0], rel[..., 1]]
        dots = jnp.einsum('bhwid,bhwjd->bhwij', q, k) * scale + bias
        ul, lr = _masks()
        dots = dots.at[:, :, -nWW].add(ul)
        dots = dots.at[:, :, nWW - 1::nWW].add(lr)
        attn = jax.nn.softmax(dots, axis=-1)
        out = jnp.einsum('bhwij,bhwjd->bhwid', attn, v)
        out = out.reshape(b, HEADS, nWH, nWW, WS, WS, HEAD_DIM)
        out = out.transpose(0, 2, 4, 3, 5, 1, 6).reshape(b, H, W, HEADS * HEAD_DIM)
        out = out @ w_out + b_out
        return jnp.roll(out, (DISP, DISP), axis=(1, 2))

    def _L0_ffn_ref(x, gate_w, gate_b, w1, w2, w3):
        import jax, jax.numpy as jnp
        import numpy as np
        D_MODEL = 64
        N_EXPERTS = 16
        HIDDEN = 128
        SCALE = 0.02
        n_experts = w1.shape[0]
        logits = jnp.einsum('bsd,de->bse', x, gate_w) + gate_b
        probs = jax.nn.softmax(logits, axis=-1)
        top_probs, top_idx = jax.lax.top_k(probs, 2)
        top_probs = top_probs / jnp.sum(top_probs, axis=-1, keepdims=True)
        dispatch = jnp.sum(jax.nn.one_hot(top_idx, n_experts, dtype=x.dtype) * top_probs[..., None], axis=-2)
        h1 = jnp.einsum('bsd,edh->bseh', x, w1)
        h2 = jnp.einsum('bsd,edh->bseh', x, w2)
        hidden = jax.nn.silu(h1) * h2
        expert_out = jnp.einsum('bseh,eho->bseo', hidden, w3)
        return jnp.einsum('bseo,bse->bso', expert_out, dispatch)

    def _L1_conv_ref(x, w1, b1, w2, b2, w3, b3):
        import jax, jax.numpy as jnp
        import numpy as np
        B, H, W, C = (16, 16, 16, 64)
        b, h, w, c = x.shape
        n = h * w
        xf = x.reshape(b, n, c)
        x0 = jnp.einsum('bnc,c->bn', xf, w1) + b1[0]
        x1 = jnp.einsum('bnc,c->bn', xf, w2) + b2[0]
        x2 = jnp.einsum('bnc,c->bn', xf, w3) + b3[0]
        sim = x0[:, :, None] * x1[:, None, :]
        sm = jax.nn.softmax(sim, axis=1)
        feats = jnp.einsum('bn,bnm->bm', x2, sm)
        gate = jax.nn.sigmoid(feats).reshape(b, h, w, 1)
        return gate * x

    def _L1_ffn_ref(x, router_w, w1, w2, w3):
        import jax, jax.numpy as jnp
        import numpy as np
        N_EXPERTS = 8
        TOP_K = 2
        B, T, C = x.shape
        flat = x.reshape(-1, C)
        logits = flat @ router_w.T
        probs = jax.nn.softmax(logits, axis=-1)
        topk_probs, topk_idx = jax.lax.top_k(probs, TOP_K)
        topk_probs = topk_probs / (jnp.sum(topk_probs, axis=-1, keepdims=True) + 1e-09)
        onehot = jax.nn.one_hot(topk_idx, N_EXPERTS, dtype=flat.dtype)
        gates = jnp.einsum('nk,nke->ne', topk_probs, onehot)
        h1 = jnp.einsum('nc,ehc->neh', flat, w1)
        h3 = jnp.einsum('nc,ehc->neh', flat, w3)
        h = jax.nn.silu(h1) * h3
        y = jnp.einsum('neh,ech->nec', h, w2)
        out = jnp.einsum('ne,nec->nc', gates, y)
        return out.reshape(B, T, C)

    def _gn(v, G=32, eps=1e-05):
        B_, H_, W_, C_ = v.shape
        g = v.reshape(B_, H_, W_, G, C_ // G)
        m = jnp.mean(g, axis=(1, 2, 4), keepdims=True)
        s = jnp.var(g, axis=(1, 2, 4), keepdims=True)
        return ((g - m) / jnp.sqrt(s + eps)).reshape(v.shape)

    def _ln_c(v, eps=1e-06):
        m = jnp.mean(v, axis=-1, keepdims=True)
        s = jnp.var(v, axis=-1, keepdims=True)
        return (v - m) / jnp.sqrt(s + eps)

    def _ln_t(v, eps=1e-05):
        m = jnp.mean(v, axis=-1, keepdims=True)
        s = jnp.var(v, axis=-1, keepdims=True)
        return (v - m) / jnp.sqrt(s + eps)

    def _to_tokens(v):
        B_, H_, W_, C_ = v.shape
        return v.reshape(B_, H_ * W_, C_)

    def _from_tokens(t, like):
        return t.reshape(like.shape)
    x = x + _L0_conv_ref(_ln_c(x), L0_conv_w_qkv, L0_conv_pos_emb, L0_conv_w_out, L0_conv_b_out)
    t = _to_tokens(x)
    t = t + _L0_ffn_ref(_ln_t(t), L0_ffn_gate_w, L0_ffn_gate_b, L0_ffn_w1, L0_ffn_w2, L0_ffn_w3)
    x = _from_tokens(t, x)
    x = x + _L1_conv_ref(_ln_c(x), L1_conv_w1, L1_conv_b1, L1_conv_w2, L1_conv_b2, L1_conv_w3, L1_conv_b3)
    t = _to_tokens(x)
    t = t + _L1_ffn_ref(_ln_t(t), L1_ffn_router_w, L1_ffn_w1, L1_ffn_w2, L1_ffn_w3)
    x = _from_tokens(t, x)
    return x

_drawn_inputs = setup_inputs


def setup_inputs(seed=0):
    import zlib

    import numpy as np

    out = dict(_drawn_inputs(seed))
    spreads = {'L0_ffn_gate_b': (0.0, 0.8)}
    factors = {'L0_ffn_gate_w': 8.0,
     'L0_ffn_w1': 8.0,
     'L0_ffn_w2': 8.0,
     'L0_ffn_w3': 8.0,
     'L1_conv_w1': 7.948,
     'L1_conv_w2': 7.198}
    for name, (base, spread) in spreads.items():
        noise = np.random.default_rng([zlib.crc32(name.encode()), seed]).standard_normal(out[name].shape)
        drawn = base * np.exp(spread * noise) if base else spread * noise
        out[name] = jnp.asarray(drawn.astype(out[name].dtype))
    for name, factor in factors.items():
        out[name] = (out[name] * factor).astype(out[name].dtype)
    return out
```

```python
from contextlib import ExitStack

import concourse.bass as bass
from concourse import mybir

F32 = mybir.dt.float32
F32R = mybir.dt.float32r
U32 = mybir.dt.uint32
I32 = mybir.dt.int32
BF16 = mybir.dt.bfloat16
ALU = mybir.AluOpType
ACT = mybir.ActivationFunctionType
AX = mybir.AxisListType

P = 128
C = 64
IMAGES = 32
WIN = 64
HEADS, HEAD_DIM = 8, 32
INNER = HEADS * HEAD_DIM
TILES = IMAGES * 2
UNIT = 4
UNITS = TILES // UNIT
PASS = 8
SCALE = HEAD_DIM ** -0.5


class Signal:
    def __init__(self, ctx, nc, name, per):
        self.sem, self.per, self.base = ctx.enter_context(nc.semaphore(name)), per, 0

    def count(self, n, k=None):
        value = self.base + n * self.per + (self.per if k is None else k)
        return max(value, 0) if isinstance(value, int) else value

    def start_over(self, steps):
        self.base += steps * self.per


def stand_alone(eng, spare):
    eng.sem_inc(spare.sem, 1)


def columns(x, n, width):
    return x[:, bass.ds(n * width, width)]


def attention_phase(nc, mem, ins, X, later):
    ctx = ExitStack()
    with ctx:
        def sb(name, shape, dt=F32):
            return ctx.enter_context(nc.sbuf_tensor(name, shape, dt))

        def pb(name):
            return ctx.enter_context(nc.psum_tensor(name, [P, 512], F32))

        used = []

        def sig(name, per=1):
            used.append(Signal(ctx, nc, "at_" + name, per))
            return used[-1]

        ident = mem["ident"]
        b_out = sb("b_out_sb", [P, 2 * C])
        wq_t = sb("wq_t_sb", [HEAD_DIM, HEADS * C])
        wk_t2 = sb("wk_t2_sb", [HEAD_DIM, HEADS * 2 * C])
        wv_blk = sb("wv_blk_sb", [P, 2 * INNER])
        w_out = sb("w_out_sb", [P, 2, C])
        rel_bias = sb("rel_bias_sb", [P, WIN])
        mask = sb("mask_sb", [P, 2, WIN])
        bias = sb("bias_sb", [P, 2, WIN])
        a_blk = sb("a_blk", [P, HEADS, P])
        stats = sb("stats", [P, 2, 6])
        mean_var = sb("mean_var", [P, 2, 2])
        var_eps, minus_mean = sb("var_eps", [P, 2]), sb("minus_mean", [P, 2])
        rstd, shift = sb("rstd", [P, 2]), sb("shift", [P, 2])
        xn = [sb(f"xn{i}", [P, 2 * C]) for i in range(2)]
        xt = [sb(f"xt{i}", [P, P]) for i in range(2)]
        xt_twice = [sb(f"xt_twice{i}", [P, 2, 2, WIN]) for i in range(2)]
        xq_blk = [sb(f"xq_blk{i}", [P, 2, P]) for i in range(2)]
        u_sb = sb("u_sb", [P, HEADS, P])
        v_blk = [[sb(f"v_blk{i}{u}", [P, 2, 4, C]) for u in range(2)] for i in range(2)]
        t_sb = [sb(f"t_sb{u}", [P, HEADS, WIN]) for u in range(2)]
        row_max = sb("row_max", [P, 2, HEADS])
        prob = [[sb(f"prob{i}{u}", [P, HEADS * WIN]) for u in range(2)] for i in range(2)]
        row_sum = [[sb(f"row_sum{i}{u}", [P, HEADS]) for u in range(2)] for i in range(2)]
        inv_sum = [[sb(f"inv_sum{i}{u}", [P, HEADS]) for u in range(2)] for i in range(2)]
        pt_sb = [sb(f"pt_sb{u}", [P, 512]) for u in range(2)]
        on_sb = [sb(f"on_sb{u}", [P, INNER]) for u in range(2)]
        ot_sb = sb("ot_sb", [P, 4, 2, WIN])
        xt_ps, u_ps, v_ps = pb("xt_ps"), [pb("u_ps0"), pb("u_ps1")], pb("v_ps")
        s_ps = [pb("s_ps0"), pb("s_ps1")]
        pt_ps = [pb("pt_ps0"), pb("pt_ps1")]

        spare = sig("spare", 0)
        loaded = sig("loaded", 0)
        zeroed = sig("zeroed", 0)
        a_made = sig("a_made", 0)
        a_kept = sig("a_kept", 0)
        bias_made = sig("bias_made", 0)
        stats_done = sig("stats_done", 4)
        rstd_done = sig("rstd_done", 4)
        xn_done = sig("xn_done", 2)
        x_biased = sig("x_biased")
        xt_done = sig("xt_done")
        xt_kept = sig("xt_kept")
        xt_spread = sig("xt_spread", 4)
        v_done = sig("v_done", 2)
        v_kept = sig("v_kept", 4)
        u_done = sig("u_done", 2)
        u_kept = sig("u_kept", 2)
        s_done = sig("s_done", 2)
        biased = sig("biased", 2)
        max_done = sig("max_done", 2)
        shifted = sig("shifted", 2)
        exp_done = sig("exp_done", 2)
        sum_done = sig("sum_done", 4)
        pt_done = sig("pt_done", 2)
        pt_kept = sig("pt_kept", 2)
        o_done = sig("o_done", 2)
        on_done = sig("on_done", 4)
        ot_done = sig("ot_done")
        ot_kept = sig("ot_kept")
        y_done = sig("y_done")
        x_added = sig("x_added")

        LOADS = [(X, "x"), (b_out, "b_out2"), (wq_t, "wq_t"), (wk_t2, "wk_t2"), (wv_blk, "wv_blk"),
                 (w_out, "w_out"), (rel_bias, "rel_bias"), (mask, "mask"), (ident, "ident")]

        with nc.Block() as block:
            @block.sync
            def _(sp):
                for tile, name in LOADS:
                    sp.dma_start(tile[:], ins[name]).then_inc(loaded.sem, 16)
                for weights in later:
                    weights.load(sp, ins)

            @block.gpsimd
            def _(pool):
                for tile, value in [(mem["minus_half"], -0.5), (mem["minus_one"], -1.0), (mem["eps6"], 1e-6),
                                    (mem["eps5"], 1e-5)]:
                    nc.gpsimd.memset(tile[:], value)
                for tile in [a_blk] + xq_blk + v_blk[0] + v_blk[1]:
                    nc.gpsimd.memset(tile[:], 0.0)

            @block.vector
            def _(dve):
                dve.wait_ge(loaded.sem, 16 * len(LOADS))
                for u in range(2):
                    nc.vector.tensor_tensor(bias[:, u], rel_bias[:], mask[:, u], ALU.add)

        with nc.Block() as block:
            @block.tensor
            def _(pe):
                for g in range(2):
                    for h in range(4):
                        head = 4 * g + h
                        last = nc.tensor.matmul(u_ps[g][:, h * C:(h + 1) * C],
                                                wk_t2[:, head * 2 * C:(head + 1) * 2 * C],
                                                wq_t[:, head * C:(head + 1) * C], start=True, stop=True)
                    last.then_inc(a_made.sem, 1)

            @block.vector
            def _(dve):
                for g in range(2):
                    dve.wait_ge(a_made.sem, g + 1)
                    for v in range(2):
                        rows = slice(v * C, (v + 1) * C)
                        nc.vector.tensor_copy(a_blk[rows, 4 * g:4 * g + 4, rows],
                                              u_ps[g][rows, 0:4 * C].rearrange("p (h c) -> p h c", h=4))

        def dve_stats(dve, n, i):
            dve.wait_ge(rstd_done.sem, rstd_done.count(n - 1))
            x = columns(X, n, 2 * C)
            for v in range(2):
                nc.vector.bn_stats(stats[:, v], x[:, v * C:(v + 1) * C]).then_inc(stats_done.sem, 1)

        def dve_mean_var(dve, n):
            dve.wait_ge(stats_done.sem, stats_done.count(n, 2))
            stand_alone(dve, spare)
            for v in range(2):
                nc.vector.bn_aggr(mean_var[:, v], stats[:, v]).then_inc(stats_done.sem, 1)

        def pool_rstd(pool, n, i):
            pool.wait_ge(stats_done.sem, stats_done.count(n))
            nc.gpsimd.tensor_tensor(var_eps[:], mean_var[:, :, 1], mem["eps6"][:, 0:2], ALU.add
                                    ).then_inc(rstd_done.sem, 1)
            pool.wait_ge(xn_done.sem, xn_done.count(n - 1))
            nc.gpsimd.tensor_tensor(minus_mean[:], mean_var[:, :, 0], mem["minus_one"][:, 0:2], ALU.mult
                                    ).then_inc(rstd_done.sem, 1)
            pool.wait_ge(rstd_done.sem, rstd_done.count(n, 1))
            nc.gpsimd.tensor_tensor(rstd[:], var_eps[:], mem["minus_half"][:, 0:2], ALU.pow
                                    ).then_inc(rstd_done.sem, 1)
            pool.wait_ge(rstd_done.sem, rstd_done.count(n, 3))
            nc.gpsimd.tensor_tensor(shift[:], minus_mean[:], rstd[:], ALU.mult).then_inc(rstd_done.sem, 1)

        def act_norm(act, n, i):
            act.wait_ge(rstd_done.sem, rstd_done.count(n))
            act.wait_ge(xt_done.sem, xt_done.count(n - 2))
            x = columns(X, n, 2 * C)
            for v in range(2):
                nc.scalar.activation(xn[i][:, v * C:(v + 1) * C], x[:, v * C:(v + 1) * C], ACT.Identity,
                                     scale=rstd[:, v:v + 1], bias=shift[:, v:v + 1]).then_inc(xn_done.sem, 1)

        def pool_bias(pool, n):
            pool.wait_ge(xn_done.sem, xn_done.count(n))
            stand_alone(pool, spare)
            x = columns(X, n, 2 * C)
            nc.gpsimd.tensor_tensor(x, x, b_out[:], ALU.add).then_inc(x_biased.sem, 1)

        def pool_shift(pool, n, u):
            pool.wait_ge(max_done.sem, max_done.count(n, u + 1))
            nc.gpsimd.tensor_tensor(t_sb[u][:], t_sb[u][:],
                                    row_max[:, u, :].unsqueeze(2).to_broadcast([P, HEADS, WIN]),
                                    ALU.subtract).then_inc(shifted.sem, 1)

        def pe_front(pe, n, i, part):
            if part == 0:
                pe.wait_ge(xn_done.sem, xn_done.count(n))
                pe.wait_ge(v_kept.sem, v_kept.count(n - 1))
                nc.tensor.transpose(xt_ps[:, 0:P], xn[i][:], ident[:]).then_inc(xt_done.sem, 1)
            if part in (3, 4):
                u = part - 3
                pe.wait_ge(xt_spread.sem, xt_spread.count(n))
                pe.wait_ge(v_kept.sem, v_kept.count(n - 1))
                nc.tensor.matmul((v_ps, xt_ps)[u][:], xt_twice[i][:, u].rearrange("p a t -> p (a t)"),
                                 wv_blk[:], start=True, stop=True).then_inc(v_done.sem, 1)
            if part in (1, 2):
                g = part - 1
                pe.wait_ge(xt_kept.sem, xt_kept.count(n))
                pe.wait_ge(u_kept.sem, u_kept.count(n - 1, g + 1))
                for h in range(4):
                    last = nc.tensor.matmul(u_ps[g][:, h * P:(h + 1) * P], a_blk[:, 4 * g + h], xt[i][:],
                                            start=True, stop=True)
                last.then_inc(u_done.sem, 1)
            if part in (5, 6):
                u = part - 5
                pe.wait_ge(u_kept.sem, u_kept.count(n))
                pe.wait_ge(on_done.sem, on_done.count(n - 1))
                nc.tensor.matmul(s_ps[u][:], xq_blk[i][:, u], u_sb[:, :, u * WIN:(u + 1) * WIN],
                                 start=True, stop=True).then_inc(s_done.sem, 1)

        def pe_back(pe, n, i, part):
            if part in (0, 1):
                u = part
                pe.wait_ge(exp_done.sem, exp_done.count(n, u + 1))
                pe.wait_ge(ot_kept.sem, ot_kept.count(n - 1))
                pe.wait_ge(x_added.sem, x_added.count(n - 1))
                for g in range(4):
                    last = nc.tensor.transpose(pt_ps[u][:, g * P:(g + 1) * P],
                                               prob[i][u][:, g * P:(g + 1) * P], ident[:])
                last.then_inc(pt_done.sem, 1)
            if part in (2, 3):
                u = part - 2
                pe.wait_ge(pt_kept.sem, pt_kept.count(n, u + 1))
                pe.wait_ge(v_kept.sem, v_kept.count(n))
                pe.wait_ge(biased.sem, biased.count(n, u + 1))
                for g in range(4):
                    last = nc.tensor.matmul(
                        s_ps[u][:].rearrange("p (v g d) -> p v g d", v=2, g=4)[:, :, g],
                        pt_sb[u][:, g * P:(g + 1) * P], v_blk[i][u][:, :, g], start=True, stop=True)
                last.then_inc(o_done.sem, 1)
            if part == 4:
                pe.wait_ge(on_done.sem, on_done.count(n))
                for u in range(2):
                    for half in range(2):
                        last = nc.tensor.transpose(pt_ps[0][:, (2 * u + half) * P:(2 * u + half + 1) * P],
                                                   on_sb[u][:, half * P:(half + 1) * P], ident[:])
                last.then_inc(ot_done.sem, 1)
            if part == 5:
                pe.wait_ge(ot_kept.sem, ot_kept.count(n))
                for v in range(2):
                    for half in range(2):
                        last = nc.tensor.matmul(pt_ps[1][:, v * C:(v + 1) * C],
                                                ot_sb[:, 2 * half + v].rearrange("p u t -> p (u t)"),
                                                w_out[:, half], start=half == 0, stop=half == 1)
                last.then_inc(y_done.sem, 1)

        def act_keep_xt(act, n, i):
            act.wait_ge(xt_done.sem, xt_done.count(n))
            act.wait_ge(u_done.sem, u_done.count(n - 2))
            act.wait_ge(xt_spread.sem, xt_spread.count(n - 2))
            nc.scalar.activation(xt[i][:], xt_ps[:, 0:P], ACT.Copy).then_inc(xt_kept.sem, 1)

        def act_keep_u(act, n, g):
            act.wait_ge(u_done.sem, u_done.count(n, g + 1))
            act.wait_ge(s_done.sem, s_done.count(n - 1))
            nc.scalar.activation(u_sb[:, 4 * g:4 * g + 4].rearrange("p h t -> p (h t)"), u_ps[g][:],
                                 ACT.Copy).then_inc(u_kept.sem, 1)

        def act_exp(act, n, i, u):
            act.wait_ge(shifted.sem, shifted.count(n, u + 1))
            act.wait_ge(pt_done.sem, pt_done.count(n - 2))
            act.wait_ge(sum_done.sem, sum_done.count(n - 2))
            nc.scalar.activation(prob[i][u][:], t_sb[u][:].rearrange("p h t -> p (h t)"),
                                 ACT.Exp).then_inc(exp_done.sem, 1)

        def act_keep_pt(act, n, u):
            act.wait_ge(pt_done.sem, pt_done.count(n, u + 1))
            act.wait_ge(o_done.sem, o_done.count(n - 1))
            nc.scalar.activation(pt_sb[u][:], pt_ps[u][:], ACT.Copy).then_inc(pt_kept.sem, 1)

        def act_keep_ot(act, n):
            act.wait_ge(ot_done.sem, ot_done.count(n))
            act.wait_ge(y_done.sem, y_done.count(n - 1))
            nc.scalar.activation(ot_sb[:].rearrange("p hv u t -> p u hv t"),
                                 pt_ps[0][:].rearrange("p (u hv t) -> p u hv t", u=2, hv=4),
                                 ACT.Copy).then_inc(ot_kept.sem, 1)

        def dve_spread_xt(dve, n, i):
            dve.wait_ge(xt_kept.sem, xt_kept.count(n))
            dve.wait_ge(s_done.sem, s_done.count(n - 2))
            dve.wait_ge(v_done.sem, v_done.count(n - 2))
            src = xt[i][:].rearrange("p (u t) -> p u t", u=2)
            for a in range(2):
                nc.vector.tensor_copy(xt_twice[i][:, :, a], src).then_inc(xt_spread.sem, 1)
            for v in range(2):
                rows = slice(v * C, (v + 1) * C)
                nc.vector.tensor_copy(xq_blk[i][rows, :, v * WIN:(v + 1) * WIN], src[rows]
                                      ).then_inc(xt_spread.sem, 1)

        def dve_keep_v(dve, n, i, u):
            dve.wait_ge(v_done.sem, v_done.count(n, u + 1))
            dve.wait_ge(o_done.sem, o_done.count(n - 2))
            for half in range(2):
                rows = slice(half * WIN, (half + 1) * WIN)
                cols = slice(half * HEAD_DIM, (half + 1) * HEAD_DIM)
                src = (v_ps, xt_ps)[u][rows].rearrange("p (vg e) -> p vg e", e=2 * HEAD_DIM)
                nc.vector.tensor_copy(v_blk[i][u][rows].rearrange("p v g e -> p (v g) e")[:, :, cols],
                                      src[:, :, cols]).then_inc(v_kept.sem, 1)

        def dve_bias_max(dve, n, u):
            dve.wait_ge(s_done.sem, s_done.count(n, u + 1))
            dve.wait_ge(exp_done.sem, exp_done.count(n - 1))
            nc.vector.scalar_tensor_tensor(out=t_sb[u][:], in0=s_ps[u][:].rearrange("p (h t) -> p h t", h=HEADS),
                                           scalar=SCALE, in1=bias[:, u].unsqueeze(1).to_broadcast([P, HEADS, WIN]),
                                           op0=ALU.mult, op1=ALU.add).then_inc(biased.sem, 1)
            dve.wait_ge(biased.sem, biased.count(n, u + 1))
            dve.wait_ge(shifted.sem, shifted.count(n - 1))
            nc.vector.tensor_reduce(row_max[:, u], t_sb[u][:], axis=AX.X, op=ALU.max).then_inc(max_done.sem, 1)

        def dve_sum(dve, n, i, u):
            dve.wait_ge(exp_done.sem, exp_done.count(n, u + 1))
            dve.wait_ge(on_done.sem, on_done.count(n - 2))
            nc.vector.tensor_reduce(row_sum[i][u][:], prob[i][u][:].rearrange("p (h t) -> p h t", h=HEADS),
                                    axis=AX.X, op=ALU.add).then_inc(sum_done.sem, 1)
            dve.wait_ge(sum_done.sem, sum_done.count(n, 2 * u + 1))
            nc.vector.reciprocal(inv_sum[i][u][:], row_sum[i][u][:]).then_inc(sum_done.sem, 1)

        def dve_normalise(dve, n, i, u):
            dve.wait_ge(o_done.sem, o_done.count(n, u + 1))
            dve.wait_ge(sum_done.sem, sum_done.count(n, 2 * u + 2))
            dve.wait_ge(ot_done.sem, ot_done.count(n - 1))
            for v in range(2):
                rows = slice(v * WIN, (v + 1) * WIN)
                nc.vector.tensor_tensor(
                    on_sb[u][rows].rearrange("p (h d) -> p h d", h=HEADS),
                    s_ps[u][rows, v * INNER:(v + 1) * INNER].rearrange("p (h d) -> p h d", h=HEADS),
                    inv_sum[i][u][rows].unsqueeze(2).to_broadcast([WIN, HEADS, HEAD_DIM]),
                    ALU.mult).then_inc(on_done.sem, 1)

        def dve_residual(dve, n):
            dve.wait_ge(y_done.sem, y_done.count(n))
            dve.wait_ge(x_biased.sem, x_biased.count(n))
            x = columns(X, n, 2 * C)
            nc.vector.tensor_tensor(x, pt_ps[1][:, 0:2 * C], x, ALU.add).then_inc(x_added.sem, 1)

        def pe_step(pe, front, f, back, b):
            if front is not None:
                for part in range(4):
                    pe_front(pe, front, f, part)
            if back is not None:
                pe_back(pe, back, b, 0)
                pe_back(pe, back, b, 1)
                pe_back(pe, back, b, 2)
                pe_back(pe, back, b, 3)
            if front is not None:
                pe_front(pe, front, f, 4)
            if back is not None:
                pe_back(pe, back, b, 4)
            if front is not None:
                pe_front(pe, front, f, 5)
                pe_front(pe, front, f, 6)
            if back is not None:
                pe_back(pe, back, b, 5)

        def act_step(act, front, f, back, b, after):
            if front is not None:
                act_keep_u(act, front, 0)
                act_keep_u(act, front, 1)
            if back is not None:
                act_keep_pt(act, back, 0)
                act_keep_pt(act, back, 1)
            if after is not None:
                act_norm(act, after, b)
            if back is not None:
                act_keep_ot(act, back)
            if after is not None:
                act_keep_xt(act, after, b)
            if front is not None:
                act_exp(act, front, f, 0)
                act_exp(act, front, f, 1)

        def dve_step(dve, front, f, back, b, after):
            if front is not None:
                dve_spread_xt(dve, front, f)
            if after is not None:
                dve_stats(dve, after, b)
            if after is not None:
                dve_mean_var(dve, after)
            if front is not None:
                dve_keep_v(dve, front, f, 0)
            if back is not None:
                dve_sum(dve, back, b, 0)
                dve_sum(dve, back, b, 1)
                dve_normalise(dve, back, b, 0)
                dve_normalise(dve, back, b, 1)
            if front is not None:
                dve_keep_v(dve, front, f, 1)
                dve_bias_max(dve, front, 0)
                dve_bias_max(dve, front, 1)
            if back is not None:
                dve_residual(dve, back)

        def pool_step(pool, front, f, after, b):
            if after is not None:
                pool_rstd(pool, after, b)
            if front is not None:
                pool_bias(pool, front)
                pool_shift(pool, front, 0)
                pool_shift(pool, front, 1)

        with nc.Block() as block:
            @block.tensor
            def _(pe):
                pe_step(pe, 0, 0, None, 1)
                pe_step(pe, 1, 1, 0, 0)
                pe_step(pe, 2, 0, 1, 1)
                with nc.tensor.Fori(1, IMAGES // 2 - 1) as k:
                    pe_step(pe, 2 * k + 1, 1, 2 * k, 0)
                    pe_step(pe, 2 * k + 2, 0, 2 * k + 1, 1)
                pe_step(pe, IMAGES - 1, 1, IMAGES - 2, 0)
                pe_step(pe, None, 0, IMAGES - 1, 1)

            @block.scalar
            def _(act):
                act_norm(act, 0, 0)
                act_keep_xt(act, 0, 0)
                act_step(act, 0, 0, None, 1, 1)
                act_step(act, 1, 1, 0, 0, 2)
                act_step(act, 2, 0, 1, 1, 3)
                with nc.scalar.Fori(1, IMAGES // 2 - 1) as k:
                    act_step(act, 2 * k + 1, 1, 2 * k, 0, 2 * k + 2)
                    act_step(act, 2 * k + 2, 0, 2 * k + 1, 1, 2 * k + 3)
                act_step(act, IMAGES - 1, 1, IMAGES - 2, 0, None)
                act_step(act, None, 0, IMAGES - 1, 1, None)

            @block.vector
            def _(dve):
                dve_stats(dve, 0, 0)
                dve_mean_var(dve, 0)
                dve_step(dve, 0, 0, None, 1, 1)
                dve_step(dve, 1, 1, 0, 0, 2)
                dve_step(dve, 2, 0, 1, 1, 3)
                with nc.vector.Fori(1, IMAGES // 2 - 1) as k:
                    dve_step(dve, 2 * k + 1, 1, 2 * k, 0, 2 * k + 2)
                    dve_step(dve, 2 * k + 2, 0, 2 * k + 1, 1, 2 * k + 3)
                dve_step(dve, IMAGES - 1, 1, IMAGES - 2, 0, None)
                dve_step(dve, None, 0, IMAGES - 1, 1, None)

            @block.gpsimd
            def _(pool):
                pool_rstd(pool, 0, 0)
                pool_step(pool, 0, 0, 1, 1)
                pool_step(pool, 1, 1, 2, 0)
                pool_step(pool, 2, 0, 3, 1)
                with nc.gpsimd.Fori(1, IMAGES // 2 - 1) as k:
                    pool_step(pool, 2 * k + 1, 1, 2 * k + 2, 0)
                    pool_step(pool, 2 * k + 2, 0, 2 * k + 3, 1)
                pool_step(pool, IMAGES - 1, 1, None, 0)
        clear(nc, used)


def clear(nc, signals):
    with nc.Block() as block:
        @block.gpsimd
        def _(pool):
            for signal in signals:
                nc.gpsimd.sem_clear(signal.sem)


class Front:

    def __init__(self, nc, ctx, mem, X, prefix, eps):
        def sb(name, shape, dt=F32):
            return ctx.enter_context(nc.sbuf_tensor(prefix + name, shape, dt))

        self.used = []

        def sig(name, per):
            self.used.append(Signal(ctx, nc, prefix + name, per))
            return self.used[-1]

        self.nc, self.mem, self.X, self.eps = nc, mem, X, mem[eps]
        self.stats = sb("stats", [P, UNIT, 6])
        self.mean_var = sb("mean_var", [P, UNIT, 2])
        self.var_eps, self.minus_mean = sb("var_eps", [P, UNIT]), sb("minus_mean", [P, UNIT])
        self.rstd, self.shift = sb("rstd", [P, UNIT]), sb("shift", [P, UNIT])
        self.xn = [sb(f"xn{i}", [P, UNIT, 2, C]) for i in range(2)]
        self.stack = [sb(f"stack{i}", [P, UNIT * P], F32R) for i in range(2)]
        self.xt_ps = ctx.enter_context(nc.psum_tensor(prefix + "xt_ps", [P, UNIT * P], F32))
        self.spare = sig("norm_spare", 0)
        self.stats_done = sig("stats_done", 2 * UNIT)
        self.rstd_done = sig("rstd_done", 4)
        self.xn_done = sig("xn_done", UNIT)
        self.xt_done = sig("xt_done", 1)
        self.hi_done = sig("hi_done", 1)
        self.stack_done = sig("stack_done", 1)
        self.xn_free = self.xt_done
        self.stack_free = None

    def dve_stats(self, dve, n):
        dve.wait_ge(self.rstd_done.sem, self.rstd_done.count(n - 1))
        stand_alone(dve, self.spare)
        x = columns(self.X, n, UNIT * C)
        for t in range(UNIT):
            self.nc.vector.bn_stats(self.stats[:, t], x[:, t * C:(t + 1) * C]).then_inc(self.stats_done.sem, 1)

    def dve_mean_var(self, dve, n):
        dve.wait_ge(self.stats_done.sem, self.stats_done.count(n, UNIT))
        stand_alone(dve, self.spare)
        for t in range(UNIT):
            self.nc.vector.bn_aggr(self.mean_var[:, t], self.stats[:, t]).then_inc(self.stats_done.sem, 1)

    def pool_rstd(self, pool, n):
        nc, mem = self.nc, self.mem
        pool.wait_ge(self.stats_done.sem, self.stats_done.count(n))
        nc.gpsimd.tensor_tensor(self.var_eps[:], self.mean_var[:, :, 1], self.eps[:], ALU.add
                                ).then_inc(self.rstd_done.sem, 1)
        pool.wait_ge(self.xn_done.sem, self.xn_done.count(n - 1))
        nc.gpsimd.tensor_tensor(self.minus_mean[:], self.mean_var[:, :, 0], mem["minus_one"][:], ALU.mult
                                ).then_inc(self.rstd_done.sem, 1)
        pool.wait_ge(self.rstd_done.sem, self.rstd_done.count(n, 1))
        nc.gpsimd.tensor_tensor(self.rstd[:], self.var_eps[:], mem["minus_half"][:], ALU.pow
                                ).then_inc(self.rstd_done.sem, 1)
        pool.wait_ge(self.rstd_done.sem, self.rstd_done.count(n, 3))
        nc.gpsimd.tensor_tensor(self.shift[:], self.minus_mean[:], self.rstd[:], ALU.mult
                                ).then_inc(self.rstd_done.sem, 1)

    def act_norm(self, act, n, i):
        act.wait_ge(self.rstd_done.sem, self.rstd_done.count(n))
        act.wait_ge(self.xn_free.sem, self.xn_free.count(n - 2))
        x = columns(self.X, n, UNIT * C)
        for t in range(UNIT):
            self.nc.scalar.activation(self.xn[i][:, t], x[:, t * C:(t + 1) * C].unsqueeze(1).to_broadcast([P, 2, C]),
                                      ACT.Identity, scale=self.rstd[:, t:t + 1], bias=self.shift[:, t:t + 1]
                                      ).then_inc(self.xn_done.sem, 1)

    def pe_transpose(self, pe, n, i):
        pe.wait_ge(self.xn_done.sem, self.xn_done.count(n))
        pe.wait_ge(self.stack_done.sem, self.stack_done.count(n - 1))
        for t in range(UNIT):
            last = self.nc.tensor.transpose(self.xt_ps[:, t * P:(t + 1) * P],
                                            self.xn[i][:, t].rearrange("p a c -> p (a c)"), self.mem["ident"][:])
        last.then_inc(self.xt_done.sem, 1)

    def act_hi(self, act, n, i):
        act.wait_ge(self.xt_done.sem, self.xt_done.count(n))
        act.wait_ge(self.stack_free.sem, self.stack_free.count(n - 2))
        self.nc.scalar.activation(self.stack[i][:], self.xt_ps[:], ACT.Copy).then_inc(self.hi_done.sem, 1)

    def dve_lo(self, dve, n, i):
        dve.wait_ge(self.hi_done.sem, self.hi_done.count(n))
        self.nc.vector.tensor_tensor(self.stack[i][C:P], self.xt_ps[C:P], self.stack[i][C:P].bitcast(F32),
                                     ALU.subtract).then_inc(self.stack_done.sem, 1)


class Split:

    def __init__(self, ctx, nc, name, cols, pieces=1):
        self.nc, self.name, self.width = nc, name, cols // pieces
        self.hi, self.lo = (ctx.enter_context(nc.sbuf_tensor(f"{name}_{x}", [P, cols], F32R)) for x in ("hi", "lo"))
        buffers = range(min(pieces, 2))
        self.raw = [ctx.enter_context(nc.sbuf_tensor(f"{name}_raw{i}", [P, self.width], F32)) for i in buffers]
        self.loaded = [Signal(ctx, nc, f"{name}_loaded{i}", 16) for i in buffers]
        self.hi_done = Signal(ctx, nc, name + "_hi_done", 1)
        self.lo_done = Signal(ctx, nc, name + "_lo_done", 1)

    def load(self, sp, ins, n=0, i=0):
        sp.wait_ge(self.lo_done.sem, self.lo_done.count(n - 2))
        sp.dma_start(self.raw[i][:], columns(ins[self.name], n, self.width)).then_inc(self.loaded[i].sem, 16)

    def act_hi(self, act, n=0, i=0, q=0):
        act.wait_ge(self.loaded[i].sem, self.loaded[i].count(q))
        self.nc.scalar.activation(columns(self.hi, n, self.width), self.raw[i][:], ACT.Copy
                                  ).then_inc(self.hi_done.sem, 1)

    def dve_lo(self, dve, n=0, i=0):
        dve.wait_ge(self.hi_done.sem, self.hi_done.count(n))
        self.nc.vector.tensor_tensor(columns(self.lo, n, self.width), self.raw[i][:],
                                     columns(self.hi, n, self.width).bitcast(F32), ALU.subtract
                                     ).then_inc(self.lo_done.sem, 1)


class Moe:

    def __init__(self, ctx, nc, prefix, experts, chunks, hidden, guard):
        def sb(name, shape, dt=F32):
            return ctx.enter_context(nc.sbuf_tensor(prefix + name, shape, dt))

        self.nc, self.prefix, self.guard = nc, prefix, guard
        self.E, self.chunks, self.hidden = experts, chunks, hidden
        self.HALF = chunks * hidden
        self.LIST = 2 * TILES + experts
        self.REGION = TILES + 1
        self.FILL = 2 * P * TILES
        self.sent = nc.dram_tensor(prefix + "sent", ((experts * self.REGION + experts) * P, C + 2), F32).ap()
        self.done = nc.dram_tensor(prefix + "done", (self.FILL + 2 * experts * P, C), F32).ap()
        self.router = Split(ctx, nc, prefix + "router", experts)
        self.w_down = sb("w_down", [hidden, experts * chunks * C])
        self.router_bias = sb("router_bias", [P, experts])
        self.number = sb("number", [P, experts])
        self.region_row = sb("region_row", [P, experts])
        self.list_number = sb("list_number", [1, self.LIST])
        self.tile_of = sb("tile_of", [1, self.LIST], I32)
        self.expert_of = sb("expert_of", [1, self.LIST], I32)
        self.loaded = ctx.enter_context(nc.semaphore(prefix + "loaded"))
        self.loads = [(self.w_down, "w_down"), (self.router_bias, "router_bias"), (self.number, "number"),
                      (self.region_row, "region_row"), (self.list_number, "list_number")]
        self.w_up = Split(ctx, nc, prefix + "w_up", experts * 2 * self.HALF, UNITS)

    def load(self, sp, ins):
        self.router.load(sp, ins)
        for tile, name in self.loads:
            sp.dma_start(tile[:], ins[self.prefix + name]).then_inc(self.loaded, 16)
        sp.dma_start(self.sent[self.E * self.REGION * P:, :], ins[self.prefix + "fill"][self.E * P:, :]
                     ).then_inc(self.loaded, 16)

    def wait_loaded(self, eng):
        eng.wait_ge(self.loaded, 16 * (len(self.loads) + 1))


class Parts:
    pass


def routing(nc, ctx, mem, ins, X, moe):
    prefix, E = moe.prefix, moe.E
    def sb(name, shape, dt=F32):
        return ctx.enter_context(nc.sbuf_tensor(prefix + name, shape, dt))

    used = []

    def sig(name, per=1):
        used.append(Signal(ctx, nc, prefix + name, per))
        return used[-1]

    def semaphore(name):
        return sig(name).sem

    front = Front(nc, ctx, mem, X, prefix, "eps5")
    logit = sb("logit", [P, UNIT, E])
    top = sb("top", [P, UNIT, 8])
    top_at = sb("top_at", [P, UNIT, 8], U32)
    top_at_f = sb("top_at_f", [P, 2, UNIT])
    below, e_second = sb("below", [P, UNIT]), sb("e_second", [P, UNIT])
    shifted, e_all = sb("shifted", [P, UNIT, E]), sb("e_all", [P, UNIT, E])
    e_sum, denom = sb("e_sum", [P, UNIT]), sb("denom", [P, UNIT])
    chosen = sb("chosen", [P, 2, UNIT, E])
    both = [sb(f"both{i}", [P, UNIT + 1, E], BF16) for i in range(2)]
    place = sb("place", [P, UNIT, E])
    slot_f = sb("slot_f", [P, 2, UNIT])
    slot = [sb(f"slot{i}", [P, 2, UNIT], U32) for i in range(2)]
    rows = [sb(f"rows{i}", [P, UNIT, 2, C + 2]) for i in range(2)]
    before, ones = sb("before", [P, P], BF16), sb("ones", [P, P], BF16)
    before_f = sb("before_f", [P, P])
    done_row = sb("done_row", [P, TILES * 2])
    fill = sb("fill", [P, E, C + 2])
    threshold = sb("threshold", [P, TILES])
    router_ps, rank_ps = (ctx.enter_context(nc.psum_tensor(prefix + x, [P, 512], F32))
                          for x in ("router_ps", "rank_ps"))

    spare = sig("spare")
    loaded = semaphore("route_loaded")
    made = semaphore("made")
    logits_done = sig("logits_done")
    logit_kept = sig("logit_kept")
    top_done = sig("top_done", 2 * UNIT + 1)
    gate_a = sig("gate_a", 2)
    gate_e = sig("gate_e", 2)
    gate_b = sig("gate_b", 5)
    chosen_done = sig("chosen_done", 2)
    both_done = sig("both_done", 2)
    ranked = sig("ranked")
    placed = sig("placed", 3)
    slots_done = sig("slots_done")
    rows_done = sig("rows_done", 2)
    sent = mem["sent"]
    front.stack_free = logits_done
    front.xn_free = rows_done

    LOADS = [(before_f, ins["before"]), (done_row, ins["done_row"]), (threshold, ins["threshold"]),
             (fill, ins[prefix + "fill"][0:E * P, :].rearrange("(e p) c -> p e c", p=P))]

    def pe_logits(pe, n, i):
        pe.wait_ge(front.stack_done.sem, front.stack_done.count(n))
        pe.wait_ge(logit_kept.sem, logit_kept.count(n - 1))
        for t in range(UNIT):
            tokens = front.stack[i][:, t * P:(t + 1) * P]
            nc.tensor.matmul(router_ps[:, t * E:(t + 1) * E], tokens, moe.router.lo[:], start=True, stop=False)
            last = nc.tensor.matmul(router_ps[:, t * E:(t + 1) * E], tokens, moe.router.hi[:],
                                    start=False, stop=True)
        last.then_inc(logits_done.sem, 1)

    def dve_top(dve, n):
        dve.wait_ge(logits_done.sem, logits_done.count(n))
        nc.vector.tensor_tensor(logit[:], router_ps[:, 0:UNIT * E].rearrange("p (t e) -> p t e", t=UNIT),
                                moe.router_bias[:].unsqueeze(1).to_broadcast([P, UNIT, E]), ALU.add
                                ).then_inc(logit_kept.sem, 1)
        dve.wait_ge(logit_kept.sem, logit_kept.count(n))
        stand_alone(dve, spare)
        for t in range(UNIT):
            nc.vector.max(top[:, t], logit[:, t]).then_inc(top_done.sem, 1)
        dve.wait_ge(top_done.sem, top_done.count(n, UNIT))
        stand_alone(dve, spare)
        for t in range(UNIT):
            nc.vector.max_index(top_at[:, t], top[:, t], logit[:, t]).then_inc(top_done.sem, 1)
        nc.vector.tensor_tensor(below[:], top[:, :, 1], top[:, :, 0], ALU.subtract).then_inc(gate_a.sem, 1)
        nc.vector.tensor_tensor(shifted[:], logit[:], top[:, :, 0:1].to_broadcast([P, UNIT, E]),
                                ALU.subtract).then_inc(gate_a.sem, 1)
        dve.wait_ge(top_done.sem, top_done.count(n, 2 * UNIT))
        nc.vector.tensor_copy(top_at_f[:].rearrange("p k t -> p t k"), top_at[:, :, 0:2]
                              ).then_inc(top_done.sem, 1)

    def dve_choose(dve, n, i):
        dve.wait_ge(top_done.sem, top_done.count(n))
        for k in range(2):
            nc.vector.tensor_tensor(chosen[:, k], moe.number[:].unsqueeze(1).to_broadcast([P, UNIT, E]),
                                    top_at_f[:, k].unsqueeze(2).to_broadcast([P, UNIT, E]), ALU.is_equal
                                    ).then_inc(chosen_done.sem, 1)
        dve.wait_ge(chosen_done.sem, chosen_done.count(n))
        nc.vector.tensor_tensor(both[i][:, 0:UNIT], chosen[:, 0], chosen[:, 1], ALU.add
                                ).then_inc(both_done.sem, 1)
        dve.wait_ge(both_done.sem, both_done.count(n, 1))
        dve.wait_ge(ranked.sem, ranked.count(n - 1))
        with nc.allow_low_precision(reason="counts up to 64, exact in bfloat16"):
            nc.vector.tensor_reduce(both[1 - i][:, UNIT], both[i][:].rearrange("p t e -> p e t"), axis=AX.X,
                                    op=ALU.add).then_inc(both_done.sem, 1)

    def pe_rank(pe, n, i):
        pe.wait_ge(both_done.sem, both_done.count(n, 1))
        pe.wait_ge(placed.sem, placed.count(n - 1, 1))
        flat = both[i][:].rearrange("p t e -> p (t e)")
        nc.tensor.matmul(rank_ps[:, 0:UNIT * E], before[:], flat[:, 0:UNIT * E], start=True, stop=False,
                         skip_group_check=True)
        for t in range(UNIT - 1):
            for later in range(t + 1, UNIT):
                nc.tensor.matmul(rank_ps[:, later * E:(later + 1) * E], ones[:], both[i][:, t],
                                 start=False, stop=False, skip_group_check=True)
        for t in range(UNIT):
            last = nc.tensor.matmul(rank_ps[:, t * E:(t + 1) * E], ones[:], both[i][:, UNIT],
                                    start=False, stop=True, skip_group_check=True)
        last.then_inc(ranked.sem, 1)

    def act_gate(act, n):
        act.wait_ge(gate_a.sem, gate_a.count(n))
        nc.scalar.activation(e_second[:], below[:], ACT.Exp).then_inc(gate_e.sem, 1)
        nc.scalar.activation(e_all[:], shifted[:], ACT.Exp).then_inc(gate_e.sem, 1)

    def dve_rows(dve, n, i, q):
        if not isinstance(q, int) or q > 0:
            dve.wait_ge(sent[i].sem, sent[i].count(q - 1))
        dve.wait_ge(front.xt_done.sem, front.xt_done.count(n))
        nc.vector.tensor_copy(rows[i][:, :, :, 0:C], front.xn[i][:, :, 0:1].to_broadcast([P, UNIT, 2, C])
                              ).then_inc(rows_done.sem, 1)
        nc.vector.tensor_copy(rows[i][:, :, :, C], columns(done_row, n, 2 * UNIT).rearrange("p (t k) -> p t k", k=2)
                              ).then_inc(rows_done.sem, 1)

    def dve_gate(dve, n, i):
        dve.wait_ge(gate_e.sem, gate_e.count(n))
        nc.vector.tensor_reduce(e_sum[:], e_all[:], axis=AX.X, op=ALU.add).then_inc(gate_b.sem, 1)
        dve.wait_ge(gate_b.sem, gate_b.count(n, 1))
        nc.vector.tensor_scalar(denom[:], e_sum[:], moe.guard, 1.0, ALU.mult, ALU.add).then_inc(gate_b.sem, 1)
        dve.wait_ge(gate_b.sem, gate_b.count(n, 2))
        nc.vector.tensor_tensor(denom[:], denom[:], e_second[:], ALU.add).then_inc(gate_b.sem, 1)
        dve.wait_ge(gate_b.sem, gate_b.count(n, 3))
        nc.vector.reciprocal(rows[i][:, :, 0, C + 1], denom[:]).then_inc(gate_b.sem, 1)
        dve.wait_ge(gate_b.sem, gate_b.count(n, 4))
        nc.vector.tensor_tensor(rows[i][:, :, 1, C + 1], rows[i][:, :, 0, C + 1], e_second[:], ALU.mult
                                ).then_inc(gate_b.sem, 1)

    def dve_slots(dve, n, i):
        dve.wait_ge(ranked.sem, ranked.count(n))
        nc.vector.tensor_tensor(place[:], rank_ps[:, 0:UNIT * E].rearrange("p (t e) -> p t e", t=UNIT),
                                moe.region_row[:].unsqueeze(1).to_broadcast([P, UNIT, E]), ALU.add
                                ).then_inc(placed.sem, 1)
        dve.wait_ge(placed.sem, placed.count(n, 1))
        nc.vector.tensor_tensor(chosen[:], chosen[:], place[:].unsqueeze(1).to_broadcast([P, 2, UNIT, E]),
                                ALU.mult).then_inc(placed.sem, 1)
        dve.wait_ge(placed.sem, placed.count(n, 2))
        nc.vector.tensor_reduce(slot_f[:], chosen[:], axis=AX.X, op=ALU.add).then_inc(placed.sem, 1)
        dve.wait_ge(placed.sem, placed.count(n))
        nc.vector.tensor_copy(slot[i][:], slot_f[:]).then_inc(slots_done.sem, 1)

    def pool_send(pool, n, i):
        pool.wait_ge(slots_done.sem, slots_done.count(n))
        pool.wait_ge(rows_done.sem, rows_done.count(n))
        pool.wait_ge(gate_b.sem, gate_b.count(n))
        stand_alone(pool, spare)
        for t in range(UNIT):
            for k in range(2):
                nc.gpsimd.indirect_dma_start(
                    out=moe.sent, out_offset=bass.IndirectOffsetOnAxis(ap=slot[i][:, k, t:t + 1], axis=0),
                    in_=rows[i][:, t, k], in_offset=None).then_inc(sent[i].sem, 16)

    def prepare():
        with nc.Block() as block:
            @block.sync
            def _(sp):
                for tile, src in LOADS:
                    sp.dma_start(tile[:], src).then_inc(loaded, 16)

            @block.gpsimd
            def _(pool):
                nc.gpsimd.memset(ones[:], 1.0)

            @block.scalar
            def _(act):
                moe.router.act_hi(act)

            @block.vector
            def _(dve):
                for i in range(2):
                    nc.vector.memset(both[i][:, UNIT], 0.0)
                moe.router.dve_lo(dve)
                moe.wait_loaded(dve)
                dve.wait_ge(loaded, 16 * len(LOADS))
                nc.vector.tensor_copy(before[:], before_f[:])

    def finish():
        with ExitStack() as ctx:
            def sb(name, shape, dt=F32):
                return ctx.enter_context(nc.sbuf_tensor(prefix + name, shape, dt))

            count = sb("count", [P, E])
            fill_f, fill_row = sb("fill_f", [P, E]), sb("fill_row", [P, E], U32)
            over = sb("over", [1, E, TILES])
            tiles_of, tiles_upto, skip, one = (sb(x, [1, E]) for x in ("tiles_of", "tiles_upto", "skip", "one"))
            behind = sb("behind", [1, moe.LIST, E])
            jump = sb("jump", [1, moe.LIST, E])
            tile_f, expert_f = sb("tile_f", [1, moe.LIST]), sb("expert_f", [1, moe.LIST])
            step, fill_at = semaphore("step"), semaphore("fill_at")
            counted = semaphore("counted")
            with nc.Block() as block:
                @block.tensor
                def _(pe):
                    nc.tensor.matmul(rank_ps[:, 0:E], ones[:], both[UNITS % 2][:, UNIT], start=True, stop=True
                                     ).then_inc(counted, 1)

                @block.vector
                def _(dve):
                    done = [0]

                    def counts(ins):
                        done[0] += 1
                        ins.then_inc(step, 1)

                    dve.wait_ge(counted, 1)
                    counts(nc.vector.tensor_copy(count[:], rank_ps[:, 0:E]))
                    counts(nc.vector.memset(one[:], 1.0))
                    dve.wait_ge(step, done[0])
                    counts(nc.vector.tensor_tensor(fill_f[:], count[:], moe.region_row[:], ALU.add))
                    dve.wait_ge(step, done[0])
                    counts(nc.vector.tensor_scalar(fill_f[:], fill_f[:], fill[:, 0, C:C + 1], -float(moe.FILL),
                                                   ALU.add, ALU.add))
                    dve.wait_ge(step, done[0])
                    nc.vector.tensor_copy(fill_row[:], fill_f[:]).then_inc(fill_at, 1)
                    counts(nc.vector.tensor_tensor(over[:], count[0:1].unsqueeze(2).to_broadcast([1, E, TILES]),
                                                   threshold[0:1].unsqueeze(1).to_broadcast([1, E, TILES]), ALU.is_gt))
                    dve.wait_ge(step, done[0])
                    counts(nc.vector.tensor_reduce(tiles_of[:], over[:], axis=AX.X, op=ALU.add))
                    dve.wait_ge(step, done[0])
                    counts(nc.vector.tensor_tensor_scan(tiles_upto[:], one[:], tiles_of[:], 0.0, ALU.mult, ALU.add))
                    counts(nc.vector.tensor_scalar(skip[:], tiles_of[:], -1.0, float(moe.REGION), ALU.mult, ALU.add))
                    dve.wait_ge(step, done[0])
                    counts(nc.vector.tensor_tensor(
                        behind[:], moe.list_number[:].unsqueeze(2).to_broadcast([1, moe.LIST, E]),
                        tiles_upto[:].unsqueeze(1).to_broadcast([1, moe.LIST, E]), ALU.is_ge))
                    dve.wait_ge(step, done[0])
                    counts(nc.vector.tensor_tensor(jump[:], behind[:], skip[:].unsqueeze(1).to_broadcast([1, moe.LIST, E]),
                                                   ALU.mult))
                    counts(nc.vector.tensor_reduce(expert_f[:], behind[:, :, 0:E - 1], axis=AX.X, op=ALU.add))
                    dve.wait_ge(step, done[0])
                    counts(nc.vector.tensor_reduce(tile_f[:], jump[:], axis=AX.X, op=ALU.add))
                    counts(nc.vector.tensor_copy(moe.expert_of[:], expert_f[:]))
                    dve.wait_ge(step, done[0])
                    counts(nc.vector.tensor_tensor(tile_f[:], tile_f[:], moe.list_number[:], ALU.add))
                    dve.wait_ge(step, done[0])
                    nc.vector.tensor_copy(moe.tile_of[:], tile_f[:])

                @block.gpsimd
                def _(pool):
                    pool.wait_ge(fill_at, 1)
                    for e in range(E):
                        nc.gpsimd.indirect_dma_start(
                            out=moe.sent, out_offset=bass.IndirectOffsetOnAxis(ap=fill_row[:, e:e + 1], axis=0),
                            in_=fill[:, e], in_offset=None).then_inc(mem["filled"].sem, 16)
                    pool.wait_ge(mem["filled"].sem, mem["filled"].count(E - 1))
                    for i in range(2):
                        pool.wait_ge(sent[i].sem, sent[i].count(UNITS // 2 - 1))
            clear(nc, used + front.used)
            for signal in sent:
                signal.start_over(UNITS // 2)
            mem["filled"].start_over(E)

    parts = Parts()
    parts.front = front
    parts.prepare = prepare
    parts.finish = finish
    parts.pe_logits = pe_logits
    parts.pe_rank = pe_rank
    parts.act_gate = act_gate
    parts.dve_top = dve_top
    parts.dve_choose = dve_choose
    parts.dve_rows = dve_rows
    parts.dve_slots = dve_slots
    parts.dve_gate = dve_gate
    parts.pool_send = pool_send
    return parts


def route_phase(nc, mem, ins, X, moe):
    with ExitStack() as ctx:
        route = routing(nc, ctx, mem, ins, X, moe)
        front = route.front

        def pe_step(pe, n, i, more=2):
            if more > 0:
                front.pe_transpose(pe, n + 1, 1 - i)
            route.pe_rank(pe, n, i)
            if more > 0:
                route.pe_logits(pe, n + 1, 1 - i)

        def act_step(act, n, i, q, more=2):
            if more > 0:
                front.act_norm(act, n + 1, 1 - i)
                front.act_hi(act, n + 1, 1 - i)
            route.act_gate(act, n)
            moe.w_up.act_hi(act, n, i, q)

        def dve_step(dve, n, i, q, more=2):
            route.dve_top(dve, n)
            if more > 0:
                front.dve_lo(dve, n + 1, 1 - i)
            route.dve_choose(dve, n, i)
            route.dve_rows(dve, n, i, q)
            if more > 1:
                front.dve_stats(dve, n + 2)
            route.dve_slots(dve, n, i)
            if more > 1:
                front.dve_mean_var(dve, n + 2)
            route.dve_gate(dve, n, i)
            moe.w_up.dve_lo(dve, n, i)

        def pool_step(pool, n, i, more=2):
            if more > 1:
                front.pool_rstd(pool, n + 2)
            route.pool_send(pool, n, i)

        route.prepare()
        LAST = UNITS - 3
        with nc.Block() as block:
            @block.sync
            def _(sp):
                moe.w_up.load(sp, ins, 0, 0)
                moe.w_up.load(sp, ins, 1, 1)
                with nc.sync.Fori(1, UNITS // 2) as k:
                    moe.w_up.load(sp, ins, 2 * k, 0)
                    moe.w_up.load(sp, ins, 2 * k + 1, 1)

            @block.tensor
            def _(pe):
                front.pe_transpose(pe, 0, 0)
                route.pe_logits(pe, 0, 0)
                for n in range(3):
                    pe_step(pe, n, n % 2)
                with nc.tensor.Fori(1, LAST // 2) as k:
                    pe_step(pe, 2 * k + 1, 1)
                    pe_step(pe, 2 * k + 2, 0)
                for n in range(LAST, UNITS):
                    pe_step(pe, n, n % 2, UNITS - 1 - n)

            @block.scalar
            def _(act):
                front.act_norm(act, 0, 0)
                front.act_hi(act, 0, 0)
                for n in range(3):
                    act_step(act, n, n % 2, n // 2)
                with nc.scalar.Fori(1, LAST // 2) as k:
                    act_step(act, 2 * k + 1, 1, k)
                    act_step(act, 2 * k + 2, 0, k + 1)
                for n in range(LAST, UNITS):
                    act_step(act, n, n % 2, n // 2, UNITS - 1 - n)

            @block.vector
            def _(dve):
                for n in range(2):
                    front.dve_stats(dve, n)
                    front.dve_mean_var(dve, n)
                front.dve_lo(dve, 0, 0)
                for n in range(3):
                    dve_step(dve, n, n % 2, n // 2)
                with nc.vector.Fori(1, LAST // 2) as k:
                    dve_step(dve, 2 * k + 1, 1, k)
                    dve_step(dve, 2 * k + 2, 0, k + 1)
                for n in range(LAST, UNITS):
                    dve_step(dve, n, n % 2, n // 2, UNITS - 1 - n)

            @block.gpsimd
            def _(pool):
                front.pool_rstd(pool, 0)
                front.pool_rstd(pool, 1)
                for n in range(3):
                    pool_step(pool, n, n % 2)
                with nc.gpsimd.Fori(1, LAST // 2) as k:
                    pool_step(pool, 2 * k + 1, 1)
                    pool_step(pool, 2 * k + 2, 0)
                for n in range(LAST, UNITS):
                    pool_step(pool, n, n % 2, UNITS - 1 - n)

        route.finish()


def experts_phase(nc, mem, X, moe, out=None, stored=None):
    prefix, E, chunks, hidden, HALF, LIST = moe.prefix, moe.E, moe.chunks, moe.hidden, moe.HALF, moe.LIST
    BANKS = -(-HALF // 512)
    SEG = HALF // BANKS
    TOGETHER = 2 * HALF <= 512
    DEPTH = 2 if TOGETHER else 1
    HT_BANKS = -(-chunks * P // 512)
    with ExitStack() as ctx:
        def sb(name, shape, dt=F32):
            return ctx.enter_context(nc.sbuf_tensor(prefix + name, shape, dt))

        def ps(name, banks=1):
            return ctx.enter_context(nc.psum_tensor(prefix + name, [P, banks, 512], F32))

        used = []

        def sig(name, per=1):
            used.append(Signal(ctx, nc, prefix + name, per))
            return used[-1]

        x_in = [sb(f"x_in{i}", [P, 2 * C + 2]) for i in range(PASS)]
        done_at = [sb(f"done_at{i}", [P, 1], U32) for i in range(PASS)]
        gate = [sb(f"gate{i}", [P, 1]) for i in range(PASS)]
        stack = [sb(f"x_stack{i}", [P, P], F32R) for i in range(2)]
        silu = [sb(f"silu{d}", [P, BANKS, SEG]) for d in range(DEPTH)]
        h_sb = [sb(f"h_sb{d}", [P, BANKS, SEG]) for d in range(DEPTH)]
        ht_sb = [sb(f"ht_sb{i}", [hidden, chunks * P]) for i in range(2)]
        y_sb = [sb(f"y_sb{i}", [P, C]) for i in range(PASS)]
        xt_ps = ps("x_t_ps")
        y_ps = [ps(f"y_ps{d}") for d in range(DEPTH)]
        if TOGETHER:
            h12_ps = [ps(f"h12_ps{d}") for d in range(DEPTH)]
            h1 = [h12_ps[d][:, :, 0:SEG] for d in range(DEPTH)]
            h2 = [h12_ps[d][:, :, SEG:2 * SEG] for d in range(DEPTH)]
        else:
            h1_ps, h2_ps = ps("h1_ps", BANKS), ps("h2_ps", BANKS)
            h1, h2 = [h1_ps[:, :, 0:SEG]], [h2_ps[:, :, 0:SEG]]
        ht_ps = [ps(f"ht_ps{d}", HT_BANKS) for d in range(DEPTH)]

        spare = sig("x_spare")
        x_loaded = [sig(f"x_loaded{i}", 32) for i in range(PASS)]
        xt_done = sig("x_t_done")
        hi_kept = sig("hi_kept")
        stack_done = sig("x_stack_done")
        h1_done, h2_done = sig("h1_done"), sig("h2_done")
        silu_done = sig("silu_done")
        h_kept = sig("h_kept")
        ht_done = sig("ht_done")
        ht_kept = sig("ht_kept")
        y_done = sig("y_done")
        ends_kept = sig("ends_kept", 2)
        y_kept = sig("y_kept")
        y_sent = mem["y_sent"]

        def load_x(sp, n, q, i):
            sp.wait_ge(xt_done.sem, xt_done.count(n - PASS))
            sp.wait_ge(ends_kept.sem, ends_kept.count(n - PASS))
            tile = sp.value_load(moe.tile_of[0:1, bass.ds(n, 1)], min_val=0, max_val=E * moe.REGION + E - 1)
            rows = moe.sent[bass.ds(tile * P, P), :]
            sp.dma_start(x_in[i][:, 0:C], rows[:, 0:C]).then_inc(x_loaded[i].sem, 16)
            sp.dma_start(x_in[i][:, C:], rows).then_inc(x_loaded[i].sem, 16)

        def pool_ends(pool, n, q, i):
            pool.wait_ge(x_loaded[i].sem, x_loaded[i].count(q))
            pool.wait_ge(y_kept.sem, y_kept.count(n - PASS))
            if not isinstance(q, int) or q > 0:
                pool.wait_ge(y_sent[i].sem, y_sent[i].count(q - 1))
            stand_alone(pool, spare)
            nc.gpsimd.tensor_copy(done_at[i][:], x_in[i][:, 2 * C:2 * C + 1]).then_inc(ends_kept.sem, 1)
            nc.gpsimd.tensor_copy(gate[i][:], x_in[i][:, 2 * C + 1:2 * C + 2]).then_inc(ends_kept.sem, 1)

        def pool_send(pool, n, q, i):
            pool.wait_ge(y_kept.sem, y_kept.count(n))
            pool.wait_ge(ends_kept.sem, ends_kept.count(n))
            stand_alone(pool, spare)
            nc.gpsimd.indirect_dma_start(
                out=moe.done, out_offset=bass.IndirectOffsetOnAxis(ap=done_at[i][:, 0:1], axis=0),
                in_=y_sb[i][:], in_offset=None).then_inc(y_sent[i].sem, 16)

        def pe_transpose(pe, n, q, i):
            pe.wait_ge(x_loaded[i].sem, x_loaded[i].count(q))
            pe.wait_ge(stack_done.sem, stack_done.count(n - 1))
            nc.tensor.transpose(xt_ps[:, 0, 0:P], x_in[i][:, 0:2 * C], mem["ident"][:]).then_inc(xt_done.sem, 1)

        def expert_of_tile(n):
            return nc.tensor.value_load(moe.expert_of[0:1, bass.ds(n, 1)], min_val=0, max_val=E - 1)

        def pe_up(pe, n, i, e):
            pe.wait_ge(stack_done.sem, stack_done.count(n))
            pe.wait_ge(h_kept.sem, h_kept.count(n - DEPTH))
            if TOGETHER:
                for w in (moe.w_up.lo, moe.w_up.hi):
                    last = nc.tensor.matmul(h12_ps[i % 2][:, 0, 0:2 * HALF], stack[i % 2][:],
                                            w[:, bass.ds(e * (2 * HALF), 2 * HALF)],
                                            start=w is moe.w_up.lo, stop=w is moe.w_up.hi)
                last.then_inc(h1_done.sem, 1)
                return
            for m, (bank, done) in enumerate(((h1_ps, h1_done), (h2_ps, h2_done))):
                for b in range(BANKS):
                    for w in (moe.w_up.lo, moe.w_up.hi):
                        last = nc.tensor.matmul(bank[:, b, 0:SEG], stack[i % 2][:],
                                                w[:, bass.ds(e * (2 * HALF) + (m * HALF + b * SEG), SEG)],
                                                start=w is moe.w_up.lo, stop=w is moe.w_up.hi)
                last.then_inc(done.sem, 1)

        def pe_transpose_h(pe, n, i):
            pe.wait_ge(h_kept.sem, h_kept.count(n))
            pe.wait_ge(ht_kept.sem, ht_kept.count(n - DEPTH))
            flat = h_sb[i % DEPTH][:].rearrange("p b s -> p (b s)")
            for c in range(chunks):
                b, at = divmod(c * P, 512)
                last = nc.tensor.transpose(ht_ps[i % DEPTH][0:hidden, b, at:at + P],
                                           flat[:, c * hidden:(c + 1) * hidden], mem["ident"][:])
            last.then_inc(ht_done.sem, 1)

        def pe_down(pe, n, i, e):
            pe.wait_ge(ht_kept.sem, ht_kept.count(n))
            pe.wait_ge(y_kept.sem, y_kept.count(n - DEPTH))
            for c in range(chunks):
                last = nc.tensor.matmul(y_ps[i % DEPTH][:, 0, 0:C], ht_sb[i % 2][:, c * P:(c + 1) * P],
                                        moe.w_down[:, bass.ds(e * (chunks * C) + c * C, C)],
                                        start=c == 0, stop=c == chunks - 1)
            last.then_inc(y_done.sem, 1)

        def act_hi(act, n, i):
            act.wait_ge(xt_done.sem, xt_done.count(n))
            act.wait_ge(h_last.sem, h_last.count(n - 2))
            nc.scalar.activation(stack[i % 2][:], xt_ps[:, 0, 0:P], ACT.Copy).then_inc(hi_kept.sem, 1)

        def dve_lo(dve, n, i):
            dve.wait_ge(hi_kept.sem, hi_kept.count(n))
            nc.vector.tensor_tensor(stack[i % 2][C:P], xt_ps[C:P, 0, 0:P], stack[i % 2][C:P].bitcast(F32),
                                    ALU.subtract).then_inc(stack_done.sem, 1)

        h_last = h1_done if TOGETHER else h2_done

        def act_silu(act, n, i):
            act.wait_ge(h1_done.sem, h1_done.count(n))
            act.wait_ge(h_kept.sem, h_kept.count(n - DEPTH))
            nc.scalar.activation(silu[i % DEPTH][:], h1[i % DEPTH], ACT.Silu).then_inc(silu_done.sem, 1)

        def dve_hidden(dve, n, i):
            dve.wait_ge(h_last.sem, h_last.count(n))
            dve.wait_ge(ht_done.sem, ht_done.count(n - DEPTH))
            dve.wait_ge(silu_done.sem, silu_done.count(n))
            nc.vector.tensor_tensor(h_sb[i % DEPTH][:], h2[i % DEPTH], silu[i % DEPTH][:], ALU.mult
                                    ).then_inc(h_kept.sem, 1)

        def act_keep_ht(act, n, i):
            act.wait_ge(ht_done.sem, ht_done.count(n))
            act.wait_ge(y_done.sem, y_done.count(n - 2))
            nc.scalar.activation(ht_sb[i % 2][:],
                                 ht_ps[i % DEPTH][0:hidden].rearrange("p b c -> p (b c)")[:, 0:chunks * P],
                                 ACT.Copy).then_inc(ht_kept.sem, 1)

        def dve_keep_y(dve, n, q, i):
            dve.wait_ge(y_done.sem, y_done.count(n))
            dve.wait_ge(ends_kept.sem, ends_kept.count(n))
            if not isinstance(q, int) or q > 0:
                dve.wait_ge(y_sent[i].sem, y_sent[i].count(q - 1))
            nc.vector.tensor_scalar(y_sb[i][:], y_ps[i % DEPTH][:, 0, 0:C], gate[i][:, 0:1], None, ALU.mult
                                    ).then_inc(y_kept.sem, 1)

        def at_step(q, i, by):
            q, i = q + (i + by) // PASS, (i + by) % PASS
            n = PASS * q + i
            return None if isinstance(n, int) and not 0 <= n < LIST else (n, q, i)

        def pe_step(pe, q, i, experts):
            if at := at_step(q, i, 0):
                experts.append(expert_of_tile(at[0]))
                pe_up(pe, at[0], at[2], experts[i])
            if at := at_step(q, i, -1):
                pe_transpose_h(pe, at[0], at[2])
            if at := at_step(q, i, 2):
                pe_transpose(pe, *at)
            if at := at_step(q, i, -2):
                pe_down(pe, at[0], at[2], experts[i - 2] if i >= 2 else expert_of_tile(at[0]))

        def act_step(act, q, i):
            if at := at_step(q, i, 0):
                act_silu(act, at[0], at[2])
            if at := at_step(q, i, -1):
                act_keep_ht(act, at[0], at[2])
            if at := at_step(q, i, 2):
                act_hi(act, at[0], at[2])

        def dve_step(dve, q, i):
            if at := at_step(q, i, -3):
                dve_keep_y(dve, *at)
            if at := at_step(q, i, 0):
                dve_hidden(dve, at[0], at[2])
            if at := at_step(q, i, 2):
                dve_lo(dve, at[0], at[2])

        def pool_step(pool, q, i):
            if at := at_step(q, i, 2):
                pool_ends(pool, *at)
            if at := at_step(q, i, -3):
                pool_send(pool, *at)

        PASSES = LIST // PASS
        with nc.Block() as block:
            @block.sync
            def _(sp):
                for i in range(PASS):
                    load_x(sp, i, 0, i)
                with nc.sync.Fori(1, PASSES) as q:
                    for i in range(PASS):
                        load_x(sp, PASS * q + i, q, i)

            @block.tensor
            def _(pe):
                for i in range(2):
                    pe_transpose(pe, i, 0, i)
                experts = []
                for i in range(PASS):
                    pe_step(pe, 0, i, experts)
                with nc.tensor.Fori(1, PASSES - 1) as q:
                    experts = []
                    for i in range(PASS):
                        pe_step(pe, q, i, experts)
                experts = []
                for i in range(PASS + 2):
                    pe_step(pe, PASSES - 1, i, experts)

            @block.scalar
            def _(act):
                for i in range(2):
                    act_hi(act, i, i)
                for i in range(PASS):
                    act_step(act, 0, i)
                with nc.scalar.Fori(1, PASSES - 1) as q:
                    for i in range(PASS):
                        act_step(act, q, i)
                for i in range(PASS + 3):
                    act_step(act, PASSES - 1, i)

            @block.vector
            def _(dve):
                for i in range(2):
                    dve_lo(dve, i, i)
                for i in range(PASS):
                    dve_step(dve, 0, i)
                with nc.vector.Fori(1, PASSES - 1) as q:
                    for i in range(PASS):
                        dve_step(dve, q, i)
                for i in range(PASS + 3):
                    dve_step(dve, PASSES - 1, i)

            @block.gpsimd
            def _(pool):
                for i in range(2):
                    pool_ends(pool, i, 0, i)
                for i in range(PASS):
                    pool_step(pool, 0, i)
                with nc.gpsimd.Fori(1, PASSES - 1) as q:
                    for i in range(PASS):
                        pool_step(pool, q, i)
                for i in range(PASS + 3):
                    pool_step(pool, PASSES - 1, i)
                for i in range(PASS):
                    pool.wait_ge(y_sent[i].sem, y_sent[i].count(PASSES - 1))
        clear(nc, used)
        for signal in y_sent:
            signal.start_over(PASSES)

    PARTS = 8
    WIDTH = TILES * C // PARTS
    with ExitStack() as ctx:
        back = ctx.enter_context(nc.sbuf_tensor(prefix + "back", [P, 2, TILES * C], F32))
        back_in = [ctx.enter_context(nc.semaphore(f"{prefix}back_in{part}")) for part in range(PARTS)]
        added = ctx.enter_context(nc.semaphore(prefix + "added"))
        with nc.Block() as block:
            @block.sync
            def _(sp):
                for part in range(PARTS):
                    for k in range(2):
                        rows = moe.done[k * P * TILES:(k + 1) * P * TILES, :].rearrange("(p t) c -> p (t c)", t=TILES)
                        cols = slice(part * WIDTH, (part + 1) * WIDTH)
                        sp.dma_start(back[:, k, cols], rows[:, cols]).then_inc(back_in[part], 16)
                if out is not None:
                    for part in range(PARTS):
                        sp.wait_ge(added, 2 * part + 2)
                        cols = slice(part * WIDTH, (part + 1) * WIDTH)
                        sp.dma_start(out[:, cols], X[:, cols]).then_inc(stored, 16)
                    sp.wait_ge(stored, 16 * PARTS)

            @block.vector
            def _(dve):
                for part in range(PARTS):
                    cols = slice(part * WIDTH, (part + 1) * WIDTH)
                    dve.wait_ge(back_in[part], 32)
                    nc.vector.tensor_tensor(X[:, cols], X[:, cols], back[:, 0, cols], ALU.add).then_inc(added, 1)
                    dve.wait_ge(added, 2 * part + 1)
                    nc.vector.tensor_tensor(X[:, cols], X[:, cols], back[:, 1, cols], ALU.add).then_inc(added, 1)


def mixing_phase(nc, mem, ins, X, moe):
    with ExitStack() as route_ctx:
        route = routing(nc, route_ctx, mem, ins, X, moe)
        mix(nc, mem, ins, X, moe, route)
        route.finish()


def mix(nc, mem, ins, X, moe, route):
    with ExitStack() as ctx:
        def sb(name, shape, dt=F32):
            return ctx.enter_context(nc.sbuf_tensor("mx_" + name, shape, dt))

        def pb(name):
            return ctx.enter_context(nc.psum_tensor("mx_" + name, [P, 512], F32))

        used = []

        def sig(name, per=1):
            used.append(Signal(ctx, nc, "mx_" + name, per))
            return used[-1]

        N = 2 * P
        front = Front(nc, ctx, mem, X, "mx_", "eps6")
        w = Split(ctx, nc, "mx_w", 2 * P + 2)
        b = sb("b", [P, 3])
        loaded = sig("loaded")
        with nc.Block() as block:
            @block.sync
            def _(sp):
                sp.dma_start(b[:], ins["mx_b"]).then_inc(loaded.sem, 16)
                w.load(sp, ins)
                moe.load(sp, ins)
                sp.wait_ge(loaded.sem, 16)

            @block.scalar
            def _(act):
                w.act_hi(act)

            @block.vector
            def _(dve):
                w.dve_lo(dve)

        x0, x2 = [sb(f"x0{i}", [P, 2, N]) for i in range(2)], [sb(f"x2{i}", [P, 2, N]) for i in range(2)]
        x1 = sb("x1", [P, 2, 2])
        most, least = sb("most", [P, 2]), sb("least", [P, 2])
        by_most, by_least = sb("by_most", [P, 2, 2]), sb("by_least", [P, 2, 2])
        bias = sb("bias", [P, 2, 2])
        weight = [sb(f"weight{i}", [P, N]) for i in range(2)]
        product = sb("product", [P, N])
        den, num, feats = sb("den", [P, UNIT]), sb("num", [P, UNIT]), sb("feats", [P, UNIT])
        e_minus, gate = sb("e_minus", [P, UNIT]), sb("gate", [P, UNIT])
        x0_ps, x2_ps, x1_ps = pb("x0_ps"), pb("x2_ps"), pb("x1_ps")

        spare = sig("spare", 0)
        up_done = sig("up_done", 3)
        x0_kept = sig("x0_kept")
        x2_kept = sig("x2_kept")
        x1_kept = sig("x1_kept")
        bound = sig("bound", 6)
        weighted = sig("weighted", UNIT)
        summed = sig("summed", UNIT)
        feats_done = sig("feats_done", 2)
        e_done = sig("e_done")
        gate_done = sig("gate_done", 2)
        x_added = sig("x_added", UNIT)
        front.stack_free = up_done
        front.xn_free = x_added

        def pe_up(pe, n, i):
            pe.wait_ge(front.stack_done.sem, front.stack_done.count(n))
            pe.wait_ge(x2_kept.sem, x2_kept.count(n - 1))
            pe.wait_ge(x0_kept.sem, x0_kept.count(n - 1))
            pe.wait_ge(x1_kept.sem, x1_kept.count(n - 1))
            for k, bank in enumerate((x0_ps, x2_ps)):
                cols = slice(k * P, (k + 1) * P)
                nc.tensor.matmul(bank[:], w.lo[:, cols], front.stack[i][:], start=True, stop=False)
                nc.tensor.matmul(bank[:], w.hi[:, cols], front.stack[i][:], start=False, stop=True
                                 ).then_inc(up_done.sem, 1)
            for t in range(UNIT):
                tokens = front.stack[i][:, t * P:(t + 1) * P]
                nc.tensor.matmul(x1_ps[:, 2 * t:2 * t + 2], tokens, w.lo[:, 2 * P:], start=True, stop=False)
                last = nc.tensor.matmul(x1_ps[:, 2 * t:2 * t + 2], tokens, w.hi[:, 2 * P:], start=False, stop=True)
            last.then_inc(up_done.sem, 1)

        def act_keep(act, n, i):
            act.wait_ge(up_done.sem, up_done.count(n, 1))
            act.wait_ge(weighted.sem, weighted.count(n - 1))
            nc.scalar.activation(x0[i][:].rearrange("p m n -> p (m n)"), x0_ps[:], ACT.Identity,
                                 bias=b[:, 0:1]).then_inc(x0_kept.sem, 1)
            act.wait_ge(up_done.sem, up_done.count(n, 2))
            act.wait_ge(summed.sem, summed.count(n - 2))
            nc.scalar.activation(x2[i][:].rearrange("p m n -> p (m n)"), x2_ps[:], ACT.Identity,
                                 bias=b[:, 2:3]).then_inc(x2_kept.sem, 1)

        def dve_bound(dve, n, i):
            dve.wait_ge(up_done.sem, up_done.count(n, 3))
            dve.wait_ge(weighted.sem, weighted.count(n - 1))
            nc.vector.tensor_scalar(x1[:].rearrange("p m v -> p (m v)"),
                                    x1_ps[:, 0:2 * UNIT].rearrange("p (t two) -> p t two", two=2)[:, :, 0],
                                    b[:, 1:2], None, ALU.add).then_inc(x1_kept.sem, 1)
            dve.wait_ge(x0_kept.sem, x0_kept.count(n))
            nc.vector.tensor_reduce(most[:], x0[i][:], axis=AX.X, op=ALU.max).then_inc(bound.sem, 1)
            nc.vector.tensor_reduce(least[:], x0[i][:], axis=AX.X, op=ALU.min).then_inc(bound.sem, 1)
            dve.wait_ge(bound.sem, bound.count(n, 2))
            dve.wait_ge(x1_kept.sem, x1_kept.count(n))
            for k, (x, y) in enumerate(((by_most, most), (by_least, least))):
                nc.vector.tensor_tensor(x[:], x1[:], y[:].unsqueeze(2).to_broadcast([P, 2, 2]), ALU.mult
                                        ).then_inc(bound.sem, 1)
            dve.wait_ge(bound.sem, bound.count(n, 4))
            nc.vector.tensor_tensor(by_most[:], by_most[:], by_least[:], ALU.max).then_inc(bound.sem, 1)
            dve.wait_ge(bound.sem, bound.count(n, 5))
            nc.vector.tensor_scalar(bias[:], by_most[:], -1.0, None, ALU.mult).then_inc(bound.sem, 1)

        def act_weigh(act, n, i, t):
            m, v = divmod(t, 2)
            if t == 0:
                act.wait_ge(bound.sem, bound.count(n))
                act.wait_ge(feats_done.sem, feats_done.count(n - 1))
            act.wait_ge(summed.sem, summed.count(n, t - 1))
            nc.scalar.activation(weight[t % 2][:], x0[i][:, m], ACT.Exp, scale=x1[:, m, v:v + 1],
                                 bias=bias[:, m, v:v + 1], accum_out=den[:, t:t + 1]).then_inc(weighted.sem, 1)

        def dve_sum(dve, n, i, t):
            dve.wait_ge(weighted.sem, weighted.count(n, t + 1))
            if t == 0:
                dve.wait_ge(x2_kept.sem, x2_kept.count(n))
            dve.wait_ge(summed.sem, summed.count(n, t))
            nc.vector.tensor_tensor_reduce(out=product[:], in0=weight[t % 2][:], in1=x2[i][:, t // 2], scale=1.0,
                                           scalar=0.0, op0=ALU.mult, op1=ALU.add, accum_out=num[:, t:t + 1]
                                           ).then_inc(summed.sem, 1)

        def dve_feats(dve, n):
            dve.wait_ge(summed.sem, summed.count(n))
            nc.vector.reciprocal(feats[:], den[:]).then_inc(feats_done.sem, 1)
            dve.wait_ge(feats_done.sem, feats_done.count(n, 1))
            nc.vector.tensor_tensor(feats[:], feats[:], num[:], ALU.mult).then_inc(feats_done.sem, 1)

        def act_sigmoid(act, n):
            act.wait_ge(feats_done.sem, feats_done.count(n))
            nc.scalar.activation(e_minus[:], feats[:], ACT.Exp, scale=-1.0).then_inc(e_done.sem, 1)

        def dve_gate(dve, n, i):
            dve.wait_ge(e_done.sem, e_done.count(n))
            nc.vector.tensor_scalar(gate[:], e_minus[:], 1.0, None, ALU.add).then_inc(gate_done.sem, 1)
            dve.wait_ge(gate_done.sem, gate_done.count(n, 1))
            nc.vector.reciprocal(gate[:], gate[:]).then_inc(gate_done.sem, 1)
            dve.wait_ge(gate_done.sem, gate_done.count(n, 2))
            for t in range(UNIT):
                x = columns(X, n, UNIT * C)[:, t * C:(t + 1) * C]
                nc.vector.scalar_tensor_tensor(out=x, in0=front.xn[i][:, t, 0], scalar=gate[:, t:t + 1], in1=x,
                                               op0=ALU.mult, op1=ALU.add).then_inc(x_added.sem, 1)

        def has(n):
            return not isinstance(n, int) or 0 <= n < UNITS

        def sp_step(sp, n, i):
            if has(n):
                moe.w_up.load(sp, ins, n, i)

        def pe_step(pe, n, i):
            if has(n):
                pe_up(pe, n, i)
            if has(n - 2):
                route.pe_rank(pe, n - 2, i)
            if has(n + 1):
                front.pe_transpose(pe, n + 1, 1 - i)
            if has(n - 1):
                route.front.pe_transpose(pe, n - 1, 1 - i)
                route.pe_logits(pe, n - 1, 1 - i)

        def act_step(act, n, i, q):
            if has(n):
                act_keep(act, n, i)
            if has(n - 2):
                route.act_gate(act, n - 2)
            if has(n + 1):
                front.act_norm(act, n + 1, 1 - i)
            if has(n - 1):
                route.front.act_norm(act, n - 1, 1 - i)
            if has(n):
                act_weigh(act, n, i, 0)
                act_weigh(act, n, i, 1)
            if has(n + 1):
                front.act_hi(act, n + 1, 1 - i)
            if has(n - 1):
                route.front.act_hi(act, n - 1, 1 - i)
            if has(n):
                act_weigh(act, n, i, 2)
                act_weigh(act, n, i, 3)
                moe.w_up.act_hi(act, n, i, q)
                act_sigmoid(act, n)

        def dve_step(dve, n, i, q):
            if has(n - 1):
                dve.wait_ge(x_added.sem, x_added.count(n - 1))
                route.front.dve_stats(dve, n - 1)
            if has(n + 2):
                front.dve_stats(dve, n + 2)
            if has(n - 2):
                route.dve_top(dve, n - 2)
            if has(n - 1):
                route.front.dve_mean_var(dve, n - 1)
            if has(n + 2):
                front.dve_mean_var(dve, n + 2)
            if has(n - 2):
                route.dve_choose(dve, n - 2, i)
            if has(n):
                dve_bound(dve, n, i)
            if has(n - 2):
                route.dve_rows(dve, n - 2, i, q - 1)
                route.dve_slots(dve, n - 2, i)
                route.dve_gate(dve, n - 2, i)
            if has(n):
                dve_sum(dve, n, i, 0)
                dve_sum(dve, n, i, 1)
            if has(n + 1):
                front.dve_lo(dve, n + 1, 1 - i)
            if has(n - 1):
                route.front.dve_lo(dve, n - 1, 1 - i)
            if has(n):
                dve_sum(dve, n, i, 2)
                dve_sum(dve, n, i, 3)
                dve_feats(dve, n)
                moe.w_up.dve_lo(dve, n, i)
                dve_gate(dve, n, i)

        def pool_step(pool, n, i):
            if has(n - 1):
                route.front.pool_rstd(pool, n - 1)
            if has(n + 2):
                front.pool_rstd(pool, n + 2)
            if has(n - 2):
                route.pool_send(pool, n - 2, i)

        route.prepare()
        FIRST, LAST = 5, UNITS - 3
        with nc.Block() as block:
            @block.sync
            def _(sp):
                for n in range(FIRST):
                    sp_step(sp, n, n % 2)
                with nc.sync.Fori(FIRST // 2, LAST // 2) as k:
                    sp_step(sp, 2 * k + 1, 1)
                    sp_step(sp, 2 * k + 2, 0)
                for n in range(LAST, UNITS + 2):
                    sp_step(sp, n, n % 2)

            @block.tensor
            def _(pe):
                front.pe_transpose(pe, 0, 0)
                for n in range(FIRST):
                    pe_step(pe, n, n % 2)
                with nc.tensor.Fori(FIRST // 2, LAST // 2) as k:
                    pe_step(pe, 2 * k + 1, 1)
                    pe_step(pe, 2 * k + 2, 0)
                for n in range(LAST, UNITS + 2):
                    pe_step(pe, n, n % 2)

            @block.scalar
            def _(act):
                front.act_norm(act, 0, 0)
                front.act_hi(act, 0, 0)
                for n in range(FIRST):
                    act_step(act, n, n % 2, n // 2)
                with nc.scalar.Fori(FIRST // 2, LAST // 2) as k:
                    act_step(act, 2 * k + 1, 1, k)
                    act_step(act, 2 * k + 2, 0, k + 1)
                for n in range(LAST, UNITS + 2):
                    act_step(act, n, n % 2, n // 2)

            @block.vector
            def _(dve):
                for n in range(2):
                    front.dve_stats(dve, n)
                    front.dve_mean_var(dve, n)
                front.dve_lo(dve, 0, 0)
                for n in range(FIRST):
                    dve_step(dve, n, n % 2, n // 2)
                with nc.vector.Fori(FIRST // 2, LAST // 2) as k:
                    dve_step(dve, 2 * k + 1, 1, k)
                    dve_step(dve, 2 * k + 2, 0, k + 1)
                for n in range(LAST, UNITS + 2):
                    dve_step(dve, n, n % 2, n // 2)

            @block.gpsimd
            def _(pool):
                front.pool_rstd(pool, 0)
                front.pool_rstd(pool, 1)
                for n in range(FIRST):
                    pool_step(pool, n, n % 2)
                with nc.gpsimd.Fori(FIRST // 2, LAST // 2) as k:
                    pool_step(pool, 2 * k + 1, 1)
                    pool_step(pool, 2 * k + 2, 0)
                for n in range(LAST, UNITS + 2):
                    pool_step(pool, n, n % 2)
        clear(nc, used + front.used)


PHASES = 4


def build(nc, ins, out):
    with ExitStack() as ctx:
        X = ctx.enter_context(nc.sbuf_tensor("X", [P, TILES * C], F32))
        mem = {"ident": ctx.enter_context(nc.sbuf_tensor("ident_sb", [P, P], F32))}
        for name in ("minus_half", "minus_one", "eps6", "eps5"):
            mem[name] = ctx.enter_context(nc.sbuf_tensor(name, [P, UNIT], F32))
        stored = ctx.enter_context(nc.semaphore("stored"))
        mem["sent"] = [Signal(ctx, nc, f"sent{i}", 16 * 2 * UNIT) for i in range(2)]
        mem["filled"] = Signal(ctx, nc, "filled", 16)
        mem["y_sent"] = [Signal(ctx, nc, f"y_sent{i}", 16) for i in range(PASS)]
        with ExitStack() as first:
            moe0 = Moe(first, nc, "m0_", experts=16, chunks=1, hidden=128, guard=0.0)
            attention_phase(nc, mem, ins, X, [moe0])
            if PHASES > 1:
                route_phase(nc, mem, ins, X, moe0)
                experts_phase(nc, mem, X, moe0)
        moe1 = Moe(ctx, nc, "m1_", experts=8, chunks=6, hidden=114, guard=1e-9)
        if PHASES > 2:
            mixing_phase(nc, mem, ins, X, moe1)
        if PHASES > 3:
            experts_phase(nc, mem, X, moe1, out, stored)
            return
        with nc.Block() as block:
            @block.sync
            def _(sp):
                sp.dma_start(out, X[:]).then_inc(stored, 16)
                sp.wait_ge(stored, 16)



def to_windows(x, np):
    x = np.roll(x, (-4, -4), axis=(1, 2))
    x = x.reshape(IMAGES, 2, 8, 2, 8, C).transpose(1, 2, 4, 0, 3, 5)
    return np.ascontiguousarray(x.reshape(P, IMAGES * 2 * C))


def from_windows(y, np):
    y = y.reshape(2, 8, 8, IMAGES, 2, C).transpose(3, 0, 1, 4, 2, 5).reshape(IMAGES, 16, 16, C)
    return np.ascontiguousarray(np.roll(y, (4, 4), axis=(1, 2)))


def lay_out(v, np):
    a = {}
    a["x"] = to_windows(v["x"], np)
    w_q, w_k, w_v = (v["L0_conv_w_qkv"][:, i * INNER:(i + 1) * INNER] for i in range(3))
    a["b_out2"] = np.tile(v["L0_conv_b_out"], (P, 2))
    a["wq_t"] = w_q.reshape(C, HEADS, HEAD_DIM).transpose(2, 1, 0).reshape(HEAD_DIM, HEADS * C)
    k_t = w_k.reshape(C, HEADS, HEAD_DIM).transpose(2, 1, 0)
    a["wk_t2"] = np.tile(k_t, (1, 1, 2)).reshape(HEAD_DIM, HEADS * 2 * C)
    blk = np.zeros((2, C, 2, INNER), w_v.dtype)
    blk[0, :, 0] = w_v
    blk[1, :, 1] = w_v
    a["wv_blk"] = blk.reshape(P, 2 * INNER)
    a["w_out"] = v["L0_conv_w_out"].reshape(2, P, C).transpose(1, 0, 2)
    t = np.arange(WIN)
    row, col = t // 8, t % 8
    rel = v["L0_conv_pos_emb"][row[None] - row[:, None] + 7, col[None] - col[:, None] + 7]
    a["rel_bias"] = np.tile(rel, (2, 1))
    lr = np.where((col[:, None] >= 4) != (col[None] >= 4), -3e38, 0.0).astype(np.float32)
    ul = np.where((row[:, None] >= 4) != (row[None] >= 4), -3e38, 0.0).astype(np.float32)
    a["mask"] = np.concatenate([np.stack([0 * ul, ul], 1), np.stack([lr, lr], 1)], 0)
    a["ident"] = np.eye(P, dtype=np.float32)
    up = np.stack([v["L0_ffn_w1"], v["L0_ffn_w2"]], 0)
    a["m0_w_up"] = np.tile(up.transpose(2, 1, 0, 3).reshape(C, -1), (2, 1))
    a["m0_w_down"] = v["L0_ffn_w3"].transpose(1, 0, 2).reshape(P, 16 * C)
    a["m0_router"] = np.tile(v["L0_ffn_gate_w"], (2, 1))
    a["m0_router_bias"] = np.tile(v["L0_ffn_gate_b"], (P, 1))
    a["m0_number"] = np.tile(np.arange(16, dtype=np.float32), (P, 1))
    cols = [np.tile(v[f"L1_conv_w{k}"][:, None], (2, w)) for k, w in ((1, P), (3, P), (2, 2))]
    a["mx_w"] = np.concatenate(cols, 1)
    a["mx_b"] = np.tile(np.concatenate([v["L1_conv_b1"], v["L1_conv_b2"], v["L1_conv_b3"]]), (P, 1))
    pad = np.zeros((2, 8, 684, C), np.float32)
    pad[0, :, :682], pad[1, :, :682] = v["L1_ffn_w1"], v["L1_ffn_w3"]
    a["m1_w_up"] = np.tile(pad.transpose(3, 1, 0, 2).reshape(C, -1), (2, 1))
    pad = np.zeros((8, C, 684), np.float32)
    pad[:, :, :682] = v["L1_ffn_w2"]
    a["m1_w_down"] = pad.reshape(8, C, 6, 114).transpose(3, 0, 2, 1).reshape(114, 48 * C)
    a["m1_router"] = np.tile(v["L1_ffn_router_w"].T, (2, 1))
    a["m1_router_bias"] = np.zeros((P, 8), np.float32)
    a["m1_number"] = np.tile(np.arange(8, dtype=np.float32), (P, 1))
    for prefix, experts in (("m0_", 16), ("m1_", 8)):
        a[prefix + "region_row"] = np.tile(P * (TILES + 1) * np.arange(experts, dtype=np.float32), (P, 1))
        a[prefix + "list_number"] = np.arange(2 * TILES + experts, dtype=np.float32)[None]
        fill = np.zeros((2 * experts * P, C + 2), np.float32)
        fill[:, C] = 2 * P * TILES + np.arange(2 * experts * P)
        a[prefix + "fill"] = fill
    a["before"] = np.triu(np.ones((P, P), np.float32), 1)
    a["threshold"] = np.tile(P * np.arange(TILES, dtype=np.float32), (P, 1))
    p, t, k = np.ogrid[0:P, 0:TILES, 0:2]
    a["done_row"] = ((k * P + p) * TILES + t).astype(np.float32).reshape(P, 2 * TILES)
    return {k: np.ascontiguousarray(x) for k, x in a.items()}


def kernel(**inputs):
    import numpy as np
    import concourse.bacc as bacc
    from concourse.bass_utils import run_bass_kernel_spmd

    arrays = lay_out({k: np.asarray(v) for k, v in inputs.items()}, np)
    nc = bacc.Bacc("TRN2", target_bir_lowering=False, num_devices=1)
    ins = {k: nc.dram_tensor("in_" + k, a.shape, F32, kind="ExternalInput").ap() for k, a in arrays.items()}
    out = nc.dram_tensor("out", (P, TILES * C), F32, kind="ExternalOutput").ap()
    build(nc, ins, out)
    r = run_bass_kernel_spmd(nc, [{"in_" + k: a for k, a in arrays.items()}], core_ids=[0])
    return from_windows(r.results[0]["out"], np)
```

```python
from contextlib import ExitStack

import concourse.bass as bass
from concourse import mybir

F32 = mybir.dt.float32
F32R = mybir.dt.float32r
U32 = mybir.dt.uint32
I32 = mybir.dt.int32
BF16 = mybir.dt.bfloat16
ALU = mybir.AluOpType
ACT = mybir.ActivationFunctionType
AX = mybir.AxisListType

P = 128
C = 64
IMAGES = 32
WIN = 64
HEADS, HEAD_DIM = 8, 32
INNER = HEADS * HEAD_DIM
TILES = IMAGES * 2
UNIT = 4
UNITS = TILES // UNIT
PASS = 8
SCALE = HEAD_DIM ** -0.5


class Signal:
    def __init__(self, ctx, nc, name, per):
        self.sem, self.per, self.base = ctx.enter_context(nc.semaphore(name)), per, 0

    def count(self, n, k=None):
        value = self.base + n * self.per + (self.per if k is None else k)
        return max(value, 0) if isinstance(value, int) else value

    def start_over(self, steps):
        self.base += steps * self.per


def stand_alone(eng, spare):
    eng.sem_inc(spare.sem, 1)


def columns(x, n, width):
    return x[:, bass.ds(n * width, width)]


def attention_phase(nc, mem, ins, X, moe):
    with ExitStack() as route_ctx:
        bank = route_ctx.enter_context(nc.psum_tensor("xt_ps", [P, 512], F32))
        route = routing(nc, route_ctx, mem, ins, X, moe, bank)
        attend(nc, mem, ins, X, moe, route, bank)
        route.finish()


def attend(nc, mem, ins, X, moe, route, xt_ps):
    with ExitStack() as ctx:
        def sb(name, shape, dt=F32):
            return ctx.enter_context(nc.sbuf_tensor(name, shape, dt))

        def pb(name):
            return ctx.enter_context(nc.psum_tensor(name, [P, 512], F32))

        used = []

        def sig(name, per=1):
            used.append(Signal(ctx, nc, "at_" + name, per))
            return used[-1]

        ident = mem["ident"]
        b_out = sb("b_out_sb", [P, 2 * C])
        wq_t = sb("wq_t_sb", [HEAD_DIM, HEADS * C])
        wk_t2 = sb("wk_t2_sb", [HEAD_DIM, HEADS * 2 * C])
        wv_blk = sb("wv_blk_sb", [P, 2 * INNER])
        w_out = sb("w_out_sb", [P, 2, C])
        rel_bias = sb("rel_bias_sb", [P, WIN])
        mask = sb("mask_sb", [P, 2, WIN])
        bias = sb("bias_sb", [P, 2, WIN])
        a_blk = sb("a_blk", [P, HEADS, P])
        stats = sb("stats", [P, 2, 6])
        mean_var = sb("mean_var", [P, 2, 2])
        var_eps, minus_mean = sb("var_eps", [P, 2]), sb("minus_mean", [P, 2])
        rstd, shift = sb("rstd", [P, 2]), sb("shift", [P, 2])
        xn = [sb(f"xn{i}", [P, 2 * C]) for i in range(2)]
        xt = [sb(f"xt{i}", [P, P]) for i in range(2)]
        xt_twice = [sb(f"xt_twice{i}", [P, 2, 2, WIN]) for i in range(2)]
        xq_blk = [sb(f"xq_blk{i}", [P, 2, P]) for i in range(2)]
        u_sb = sb("u_sb", [P, HEADS, P])
        v_blk = [[sb(f"v_blk{i}{u}", [P, 2, 4, C]) for u in range(2)] for i in range(2)]
        t_sb = [sb(f"t_sb{u}", [P, HEADS, WIN]) for u in range(2)]
        row_max = sb("row_max", [P, 2, HEADS])
        prob = [[sb(f"prob{i}{u}", [P, HEADS * WIN]) for u in range(2)] for i in range(2)]
        row_sum = [[sb(f"row_sum{i}{u}", [P, HEADS]) for u in range(2)] for i in range(2)]
        inv_sum = [[sb(f"inv_sum{i}{u}", [P, HEADS]) for u in range(2)] for i in range(2)]
        pt_sb = [sb(f"pt_sb{u}", [P, 512]) for u in range(2)]
        on_sb = [sb(f"on_sb{u}", [P, INNER]) for u in range(2)]
        ot_sb = sb("ot_sb", [P, 4, 2, WIN])
        u_ps, v_ps = [pb("u_ps0"), pb("u_ps1")], pb("v_ps")
        s_ps = [pb("s_ps0"), pb("s_ps1")]
        pt_ps = [pb("pt_ps0"), pb("pt_ps1")]

        spare = sig("spare", 0)
        loaded = sig("loaded", 0)
        a_made = sig("a_made", 0)
        stats_done = sig("stats_done", 4)
        rstd_done = sig("rstd_done", 4)
        xn_done = sig("xn_done", 2)
        x_biased = sig("x_biased")
        xt_done = sig("xt_done")
        xt_kept = sig("xt_kept")
        xt_spread = sig("xt_spread", 4)
        v_done = sig("v_done", 2)
        v_kept = sig("v_kept", 4)
        u_done = sig("u_done", 2)
        u_kept = sig("u_kept", 2)
        s_done = sig("s_done", 2)
        biased = sig("biased", 2)
        max_done = sig("max_done", 2)
        shifted = sig("shifted", 2)
        exp_done = sig("exp_done", 2)
        sum_done = sig("sum_done", 4)
        pt_done = sig("pt_done", 2)
        pt_kept = sig("pt_kept", 2)
        o_done = sig("o_done", 2)
        on_done = sig("on_done", 4)
        ot_done = sig("ot_done")
        ot_kept = sig("ot_kept")
        y_done = sig("y_done")
        x_added = sig("x_added")

        LOADS = [(X, "x"), (b_out, "b_out2"), (wq_t, "wq_t"), (wk_t2, "wk_t2"), (wv_blk, "wv_blk"),
                 (w_out, "w_out"), (rel_bias, "rel_bias"), (mask, "mask"), (ident, "ident")]

        with nc.Block() as block:
            @block.sync
            def _(sp):
                for tile, name in LOADS:
                    sp.dma_start(tile[:], ins[name]).then_inc(loaded.sem, 16)
                moe.load(sp, ins)

            @block.gpsimd
            def _(pool):
                for tile, value in [(mem["minus_half"], -0.5), (mem["minus_one"], -1.0), (mem["eps6"], 1e-6),
                                    (mem["eps5"], 1e-5)]:
                    nc.gpsimd.memset(tile[:], value)
                for tile in [a_blk] + xq_blk + v_blk[0] + v_blk[1]:
                    nc.gpsimd.memset(tile[:], 0.0)

            @block.vector
            def _(dve):
                dve.wait_ge(loaded.sem, 16 * len(LOADS))
                for u in range(2):
                    nc.vector.tensor_tensor(bias[:, u], rel_bias[:], mask[:, u], ALU.add)

        with nc.Block() as block:
            @block.tensor
            def _(pe):
                for g in range(2):
                    for h in range(4):
                        head = 4 * g + h
                        last = nc.tensor.matmul(u_ps[g][:, h * C:(h + 1) * C],
                                                wk_t2[:, head * 2 * C:(head + 1) * 2 * C],
                                                wq_t[:, head * C:(head + 1) * C], start=True, stop=True)
                    last.then_inc(a_made.sem, 1)

            @block.vector
            def _(dve):
                for g in range(2):
                    dve.wait_ge(a_made.sem, g + 1)
                    for v in range(2):
                        rows = slice(v * C, (v + 1) * C)
                        nc.vector.tensor_copy(a_blk[rows, 4 * g:4 * g + 4, rows],
                                              u_ps[g][rows, 0:4 * C].rearrange("p (h c) -> p h c", h=4))

        def dve_stats(dve, n, i):
            dve.wait_ge(rstd_done.sem, rstd_done.count(n - 1))
            x = columns(X, n, 2 * C)
            for v in range(2):
                nc.vector.bn_stats(stats[:, v], x[:, v * C:(v + 1) * C]).then_inc(stats_done.sem, 1)

        def dve_mean_var(dve, n):
            dve.wait_ge(stats_done.sem, stats_done.count(n, 2))
            stand_alone(dve, spare)
            for v in range(2):
                nc.vector.bn_aggr(mean_var[:, v], stats[:, v]).then_inc(stats_done.sem, 1)

        def pool_rstd(pool, n, i):
            pool.wait_ge(stats_done.sem, stats_done.count(n))
            nc.gpsimd.tensor_tensor(var_eps[:], mean_var[:, :, 1], mem["eps6"][:, 0:2], ALU.add
                                    ).then_inc(rstd_done.sem, 1)
            pool.wait_ge(xn_done.sem, xn_done.count(n - 1))
            nc.gpsimd.tensor_tensor(minus_mean[:], mean_var[:, :, 0], mem["minus_one"][:, 0:2], ALU.mult
                                    ).then_inc(rstd_done.sem, 1)
            pool.wait_ge(rstd_done.sem, rstd_done.count(n, 1))
            nc.gpsimd.tensor_tensor(rstd[:], var_eps[:], mem["minus_half"][:, 0:2], ALU.pow
                                    ).then_inc(rstd_done.sem, 1)
            pool.wait_ge(rstd_done.sem, rstd_done.count(n, 3))
            nc.gpsimd.tensor_tensor(shift[:], minus_mean[:], rstd[:], ALU.mult).then_inc(rstd_done.sem, 1)

        def act_norm(act, n, i):
            act.wait_ge(rstd_done.sem, rstd_done.count(n))
            act.wait_ge(xt_done.sem, xt_done.count(n - 2))
            x = columns(X, n, 2 * C)
            for v in range(2):
                nc.scalar.activation(xn[i][:, v * C:(v + 1) * C], x[:, v * C:(v + 1) * C], ACT.Identity,
                                     scale=rstd[:, v:v + 1], bias=shift[:, v:v + 1]).then_inc(xn_done.sem, 1)

        def pool_bias(pool, n):
            pool.wait_ge(xn_done.sem, xn_done.count(n))
            stand_alone(pool, spare)
            x = columns(X, n, 2 * C)
            nc.gpsimd.tensor_tensor(x, x, b_out[:], ALU.add).then_inc(x_biased.sem, 1)

        def pool_shift(pool, n, u):
            pool.wait_ge(max_done.sem, max_done.count(n, u + 1))
            nc.gpsimd.tensor_tensor(t_sb[u][:], t_sb[u][:],
                                    row_max[:, u, :].unsqueeze(2).to_broadcast([P, HEADS, WIN]),
                                    ALU.subtract).then_inc(shifted.sem, 1)

        def pe_front(pe, n, i, part):
            if part == 0:
                pe.wait_ge(xn_done.sem, xn_done.count(n))
                nc.tensor.transpose(xt_ps[:, 0:P], xn[i][:], ident[:]).then_inc(xt_done.sem, 1)
            if part in (3, 4):
                u = part - 3
                pe.wait_ge(xt_spread.sem, xt_spread.count(n))
                pe.wait_ge(v_kept.sem, v_kept.count(n - 1 + u, 4 - 2 * u))
                nc.tensor.matmul(v_ps[:], xt_twice[i][:, u].rearrange("p a t -> p (a t)"),
                                 wv_blk[:], start=True, stop=True).then_inc(v_done.sem, 1)
            if part in (1, 2):
                g = part - 1
                pe.wait_ge(xt_kept.sem, xt_kept.count(n))
                pe.wait_ge(u_kept.sem, u_kept.count(n - 1, g + 1))
                for h in range(4):
                    last = nc.tensor.matmul(u_ps[g][:, h * P:(h + 1) * P], a_blk[:, 4 * g + h], xt[i][:],
                                            start=True, stop=True)
                last.then_inc(u_done.sem, 1)
            if part in (5, 6):
                u = part - 5
                pe.wait_ge(u_kept.sem, u_kept.count(n))
                pe.wait_ge(on_done.sem, on_done.count(n - 1))
                nc.tensor.matmul(s_ps[u][:], xq_blk[i][:, u], u_sb[:, :, u * WIN:(u + 1) * WIN],
                                 start=True, stop=True).then_inc(s_done.sem, 1)

        def pe_back(pe, n, i, part):
            if part in (0, 1):
                u = part
                pe.wait_ge(exp_done.sem, exp_done.count(n, u + 1))
                pe.wait_ge(ot_kept.sem, ot_kept.count(n - 1))
                pe.wait_ge(x_added.sem, x_added.count(n - 1))
                for g in range(4):
                    last = nc.tensor.transpose(pt_ps[u][:, g * P:(g + 1) * P],
                                               prob[i][u][:, g * P:(g + 1) * P], ident[:])
                last.then_inc(pt_done.sem, 1)
            if part in (2, 3):
                u = part - 2
                pe.wait_ge(pt_kept.sem, pt_kept.count(n, u + 1))
                pe.wait_ge(v_kept.sem, v_kept.count(n))
                pe.wait_ge(biased.sem, biased.count(n, u + 1))
                for g in range(4):
                    last = nc.tensor.matmul(
                        s_ps[u][:].rearrange("p (v g d) -> p v g d", v=2, g=4)[:, :, g],
                        pt_sb[u][:, g * P:(g + 1) * P], v_blk[i][u][:, :, g], start=True, stop=True)
                last.then_inc(o_done.sem, 1)
            if part == 4:
                pe.wait_ge(on_done.sem, on_done.count(n))
                for u in range(2):
                    for half in range(2):
                        last = nc.tensor.transpose(pt_ps[0][:, (2 * u + half) * P:(2 * u + half + 1) * P],
                                                   on_sb[u][:, half * P:(half + 1) * P], ident[:])
                last.then_inc(ot_done.sem, 1)
            if part == 5:
                pe.wait_ge(ot_kept.sem, ot_kept.count(n))
                for v in range(2):
                    for half in range(2):
                        last = nc.tensor.matmul(pt_ps[1][:, v * C:(v + 1) * C],
                                                ot_sb[:, 2 * half + v].rearrange("p u t -> p (u t)"),
                                                w_out[:, half], start=half == 0, stop=half == 1)
                last.then_inc(y_done.sem, 1)

        def act_keep_xt(act, n, i):
            act.wait_ge(xt_done.sem, xt_done.count(n))
            act.wait_ge(u_done.sem, u_done.count(n - 2))
            act.wait_ge(xt_spread.sem, xt_spread.count(n - 2))
            nc.scalar.activation(xt[i][:], xt_ps[:, 0:P], ACT.Copy).then_inc(xt_kept.sem, 1)

        def act_keep_u(act, n, g):
            act.wait_ge(u_done.sem, u_done.count(n, g + 1))
            act.wait_ge(s_done.sem, s_done.count(n - 1))
            nc.scalar.activation(u_sb[:, 4 * g:4 * g + 4].rearrange("p h t -> p (h t)"), u_ps[g][:],
                                 ACT.Copy).then_inc(u_kept.sem, 1)

        def act_exp(act, n, i, u):
            act.wait_ge(shifted.sem, shifted.count(n, u + 1))
            act.wait_ge(pt_done.sem, pt_done.count(n - 2))
            act.wait_ge(sum_done.sem, sum_done.count(n - 2))
            nc.scalar.activation(prob[i][u][:], t_sb[u][:].rearrange("p h t -> p (h t)"),
                                 ACT.Exp).then_inc(exp_done.sem, 1)

        def act_keep_pt(act, n, u):
            act.wait_ge(pt_done.sem, pt_done.count(n, u + 1))
            act.wait_ge(o_done.sem, o_done.count(n - 1))
            nc.scalar.activation(pt_sb[u][:], pt_ps[u][:], ACT.Copy).then_inc(pt_kept.sem, 1)

        def act_keep_ot(act, n):
            act.wait_ge(ot_done.sem, ot_done.count(n))
            act.wait_ge(y_done.sem, y_done.count(n - 1))
            nc.scalar.activation(ot_sb[:].rearrange("p hv u t -> p u hv t"),
                                 pt_ps[0][:].rearrange("p (u hv t) -> p u hv t", u=2, hv=4),
                                 ACT.Copy).then_inc(ot_kept.sem, 1)

        def dve_spread_xt(dve, n, i):
            dve.wait_ge(xt_kept.sem, xt_kept.count(n))
            dve.wait_ge(s_done.sem, s_done.count(n - 2))
            dve.wait_ge(v_done.sem, v_done.count(n - 2))
            src = xt[i][:].rearrange("p (u t) -> p u t", u=2)
            for a in range(2):
                nc.vector.tensor_copy(xt_twice[i][:, :, a], src).then_inc(xt_spread.sem, 1)
            for v in range(2):
                rows = slice(v * C, (v + 1) * C)
                nc.vector.tensor_copy(xq_blk[i][rows, :, v * WIN:(v + 1) * WIN], src[rows]
                                      ).then_inc(xt_spread.sem, 1)

        def dve_keep_v(dve, n, i, u):
            dve.wait_ge(v_done.sem, v_done.count(n, u + 1))
            dve.wait_ge(o_done.sem, o_done.count(n - 2))
            for half in range(2):
                rows = slice(half * WIN, (half + 1) * WIN)
                cols = slice(half * HEAD_DIM, (half + 1) * HEAD_DIM)
                src = v_ps[rows].rearrange("p (vg e) -> p vg e", e=2 * HEAD_DIM)
                nc.vector.tensor_copy(v_blk[i][u][rows].rearrange("p v g e -> p (v g) e")[:, :, cols],
                                      src[:, :, cols]).then_inc(v_kept.sem, 1)

        def dve_bias_max(dve, n, u):
            dve.wait_ge(s_done.sem, s_done.count(n, u + 1))
            dve.wait_ge(exp_done.sem, exp_done.count(n - 1))
            nc.vector.scalar_tensor_tensor(out=t_sb[u][:], in0=s_ps[u][:].rearrange("p (h t) -> p h t", h=HEADS),
                                           scalar=SCALE, in1=bias[:, u].unsqueeze(1).to_broadcast([P, HEADS, WIN]),
                                           op0=ALU.mult, op1=ALU.add).then_inc(biased.sem, 1)
            dve.wait_ge(biased.sem, biased.count(n, u + 1))
            dve.wait_ge(shifted.sem, shifted.count(n - 1))
            nc.vector.tensor_reduce(row_max[:, u], t_sb[u][:], axis=AX.X, op=ALU.max).then_inc(max_done.sem, 1)

        def dve_sum(dve, n, i, u):
            dve.wait_ge(exp_done.sem, exp_done.count(n, u + 1))
            dve.wait_ge(on_done.sem, on_done.count(n - 2))
            nc.vector.tensor_reduce(row_sum[i][u][:], prob[i][u][:].rearrange("p (h t) -> p h t", h=HEADS),
                                    axis=AX.X, op=ALU.add).then_inc(sum_done.sem, 1)
            dve.wait_ge(sum_done.sem, sum_done.count(n, 2 * u + 1))
            nc.vector.reciprocal(inv_sum[i][u][:], row_sum[i][u][:]).then_inc(sum_done.sem, 1)

        def dve_normalise(dve, n, i, u):
            dve.wait_ge(o_done.sem, o_done.count(n, u + 1))
            dve.wait_ge(sum_done.sem, sum_done.count(n, 2 * u + 2))
            dve.wait_ge(ot_done.sem, ot_done.count(n - 1))
            for v in range(2):
                rows = slice(v * WIN, (v + 1) * WIN)
                nc.vector.tensor_tensor(
                    on_sb[u][rows].rearrange("p (h d) -> p h d", h=HEADS),
                    s_ps[u][rows, v * INNER:(v + 1) * INNER].rearrange("p (h d) -> p h d", h=HEADS),
                    inv_sum[i][u][rows].unsqueeze(2).to_broadcast([WIN, HEADS, HEAD_DIM]),
                    ALU.mult).then_inc(on_done.sem, 1)

        def dve_residual(dve, n):
            dve.wait_ge(y_done.sem, y_done.count(n))
            dve.wait_ge(x_biased.sem, x_biased.count(n))
            x = columns(X, n, 2 * C)
            nc.vector.tensor_tensor(x, pt_ps[1][:, 0:2 * C], x, ALU.add).then_inc(x_added.sem, 1)

        def has(m):
            return not isinstance(m, int) or 0 <= m < IMAGES

        def units(k, j):
            def unit(by):
                ahead, odd = divmod(3 + j - by, 2)
                r = 2 * k + ahead
                return None if odd or isinstance(r, int) and not 0 <= r < UNITS else (r, ahead % 2, k + ahead // 2)
            return 4 * k + 3 + j, (3 + j) % 2, unit

        def sp_step(sp, k, j):
            m, i, unit = units(k, j)
            if at := unit(6):
                moe.w_up.load(sp, ins, at[0], at[1])

        def pe_step(pe, k, j):
            m, i, unit = units(k, j)
            if at := unit(5):
                pe.wait_ge(route.logit_kept.sem, route.logit_kept.count(at[0]))
            if at := unit(6):
                pe.wait_ge(route.placed.sem, route.placed.count(at[0], 1))
            if has(m):
                for part in range(4):
                    pe_front(pe, m, i, part)
            if has(m - 1):
                for part in range(2):
                    pe_back(pe, m - 1, 1 - i, part)
            if at := unit(4):
                route.front.pe_transpose(pe, at[0], at[1])
            if has(m - 1):
                for part in range(2, 4):
                    pe_back(pe, m - 1, 1 - i, part)
            if has(m):
                pe_front(pe, m, i, 4)
            if has(m - 1):
                pe_back(pe, m - 1, 1 - i, 4)
            if at := unit(4):
                route.pe_logits(pe, at[0], at[1])
            if at := unit(5):
                route.pe_rank(pe, at[0], at[1])
            if has(m):
                pe_front(pe, m, i, 5)
                pe_front(pe, m, i, 6)
            if has(m - 1):
                pe_back(pe, m - 1, 1 - i, 5)

        def act_step(act, k, j):
            m, i, unit = units(k, j)
            if has(m):
                act_keep_u(act, m, 0)
                act_keep_u(act, m, 1)
            if has(m - 1):
                act_keep_pt(act, m - 1, 0)
                act_keep_pt(act, m - 1, 1)
            if at := unit(4):
                route.front.act_hi(act, at[0], at[1])
            if has(m - 1):
                act_keep_ot(act, m - 1)
            if has(m + 1):
                act_norm(act, m + 1, 1 - i)
            if at := unit(5):
                route.act_gate(act, at[0])
            if has(m + 1):
                act_keep_xt(act, m + 1, 1 - i)
            if has(m):
                act_exp(act, m, i, 0)
                act_exp(act, m, i, 1)
            if at := unit(3):
                route.front.act_norm(act, at[0], at[1])
            if at := unit(6):
                moe.w_up.act_hi(act, *at)

        def dve_step(dve, k, j):
            m, i, unit = units(k, j)
            if has(m):
                dve_spread_xt(dve, m, i)
            if has(m + 1):
                dve_stats(dve, m + 1, 1 - i)
                dve_mean_var(dve, m + 1)
            if at := unit(5):
                route.dve_top(dve, at[0])
            if has(m):
                dve_keep_v(dve, m, i, 0)
            if at := unit(7):
                moe.w_up.dve_lo(dve, at[0], at[1])
            if at := unit(5):
                route.dve_choose(dve, at[0], at[1])
            if at := unit(6):
                route.dve_rows(dve, at[0], at[1])
                route.dve_gate(dve, at[0], at[1])
            if has(m - 1):
                dve_sum(dve, m - 1, 1 - i, 0)
                dve_sum(dve, m - 1, 1 - i, 1)
            if at := unit(4):
                route.front.dve_lo(dve, at[0], at[1])
            if has(m - 1):
                dve_normalise(dve, m - 1, 1 - i, 0)
                dve_normalise(dve, m - 1, 1 - i, 1)
            if has(m):
                dve_keep_v(dve, m, i, 1)
            if at := unit(4):
                route.dve_logits(dve, at[0])
            if at := unit(5):
                route.dve_room(dve, at[1], at[2])
                route.dve_slots(dve, at[0], at[1])
            if has(m):
                dve_bias_max(dve, m, 0)
                dve_bias_max(dve, m, 1)
            if has(m - 1):
                dve_residual(dve, m - 1)
            if at := unit(3):
                dve.wait_ge(x_added.sem, x_added.count(2 * at[0] + 1))
                route.front.dve_stats(dve, at[0])
                route.front.dve_mean_var(dve, at[0])

        def pool_step(pool, k, j):
            m, i, unit = units(k, j)
            if has(m + 1):
                pool_rstd(pool, m + 1, 1 - i)
            if has(m):
                pool_bias(pool, m)
                pool_shift(pool, m, 0)
                pool_shift(pool, m, 1)
            if at := unit(3):
                route.front.pool_rstd(pool, at[0])
            if at := unit(7):
                route.pool_send(pool, at[0], at[1], range(UNIT // 2, UNIT))
            if at := unit(6):
                route.pool_send(pool, at[0], at[1], range(UNIT // 2))

        BEFORE = [divmod(m - 3, 4) for m in range(11)]
        PASSES = (2, (IMAGES - 5) // 4 + 1)
        AFTER = [divmod(m - 3, 4) for m in range(4 * PASSES[1] + 3, IMAGES + 6)]
        route.prepare()
        with nc.Block() as block:
            @block.sync
            def _(sp):
                for k, j in BEFORE:
                    sp_step(sp, k, j)
                with nc.sync.Fori(*PASSES) as k:
                    for j in range(4):
                        sp_step(sp, k, j)
                for k, j in AFTER:
                    sp_step(sp, k, j)

            @block.tensor
            def _(pe):
                for k, j in BEFORE:
                    pe_step(pe, k, j)
                with nc.tensor.Fori(*PASSES) as k:
                    for j in range(4):
                        pe_step(pe, k, j)
                for k, j in AFTER:
                    pe_step(pe, k, j)

            @block.scalar
            def _(act):
                act_norm(act, 0, 0)
                act_keep_xt(act, 0, 0)
                for k, j in BEFORE:
                    act_step(act, k, j)
                with nc.scalar.Fori(*PASSES) as k:
                    for j in range(4):
                        act_step(act, k, j)
                for k, j in AFTER:
                    act_step(act, k, j)

            @block.vector
            def _(dve):
                dve_stats(dve, 0, 0)
                dve_mean_var(dve, 0)
                for k, j in BEFORE:
                    dve_step(dve, k, j)
                with nc.vector.Fori(*PASSES) as k:
                    for j in range(4):
                        dve_step(dve, k, j)
                for k, j in AFTER:
                    dve_step(dve, k, j)

            @block.gpsimd
            def _(pool):
                pool_rstd(pool, 0, 0)
                for k, j in BEFORE:
                    pool_step(pool, k, j)
                with nc.gpsimd.Fori(*PASSES) as k:
                    for j in range(4):
                        pool_step(pool, k, j)
                for k, j in AFTER:
                    pool_step(pool, k, j)

        clear(nc, used)


def clear(nc, signals):
    with nc.Block() as block:
        @block.gpsimd
        def _(pool):
            for signal in signals:
                nc.gpsimd.sem_clear(signal.sem)


class Front:

    def __init__(self, nc, ctx, mem, X, prefix, eps, bank=None):
        def sb(name, shape, dt=F32):
            return ctx.enter_context(nc.sbuf_tensor(prefix + name, shape, dt))

        self.used = []

        def sig(name, per):
            self.used.append(Signal(ctx, nc, prefix + name, per))
            return self.used[-1]

        self.nc, self.mem, self.X, self.eps = nc, mem, X, mem[eps]
        self.stats = sb("stats", [P, UNIT, 6])
        self.mean_var = sb("mean_var", [P, UNIT, 2])
        self.var_eps, self.minus_mean = sb("var_eps", [P, UNIT]), sb("minus_mean", [P, UNIT])
        self.rstd, self.shift = sb("rstd", [P, UNIT]), sb("shift", [P, UNIT])
        self.xn = [sb(f"xn{i}", [P, UNIT, 2, C]) for i in range(2)]
        self.stack = [sb(f"stack{i}", [P, UNIT * P], F32R) for i in range(2)]
        self.xt_ps = bank or ctx.enter_context(nc.psum_tensor(prefix + "xt_ps", [P, UNIT * P], F32))
        self.spare = sig("norm_spare", 0)
        self.stats_done = sig("stats_done", 2 * UNIT)
        self.rstd_done = sig("rstd_done", 4)
        self.xn_done = sig("xn_done", UNIT)
        self.xt_done = sig("xt_done", 1)
        self.hi_done = sig("hi_done", 1)
        self.stack_done = sig("stack_done", 1)
        self.xn_free = self.xt_done
        self.stack_free = None

    def dve_stats(self, dve, n):
        dve.wait_ge(self.rstd_done.sem, self.rstd_done.count(n - 1))
        stand_alone(dve, self.spare)
        x = columns(self.X, n, UNIT * C)
        for t in range(UNIT):
            self.nc.vector.bn_stats(self.stats[:, t], x[:, t * C:(t + 1) * C]).then_inc(self.stats_done.sem, 1)

    def dve_mean_var(self, dve, n):
        dve.wait_ge(self.stats_done.sem, self.stats_done.count(n, UNIT))
        stand_alone(dve, self.spare)
        for t in range(UNIT):
            self.nc.vector.bn_aggr(self.mean_var[:, t], self.stats[:, t]).then_inc(self.stats_done.sem, 1)

    def pool_rstd(self, pool, n):
        nc, mem = self.nc, self.mem
        pool.wait_ge(self.stats_done.sem, self.stats_done.count(n))
        nc.gpsimd.tensor_tensor(self.var_eps[:], self.mean_var[:, :, 1], self.eps[:], ALU.add
                                ).then_inc(self.rstd_done.sem, 1)
        pool.wait_ge(self.xn_done.sem, self.xn_done.count(n - 1))
        nc.gpsimd.tensor_tensor(self.minus_mean[:], self.mean_var[:, :, 0], mem["minus_one"][:], ALU.mult
                                ).then_inc(self.rstd_done.sem, 1)
        pool.wait_ge(self.rstd_done.sem, self.rstd_done.count(n, 1))
        nc.gpsimd.tensor_tensor(self.rstd[:], self.var_eps[:], mem["minus_half"][:], ALU.pow
                                ).then_inc(self.rstd_done.sem, 1)
        pool.wait_ge(self.rstd_done.sem, self.rstd_done.count(n, 3))
        nc.gpsimd.tensor_tensor(self.shift[:], self.minus_mean[:], self.rstd[:], ALU.mult
                                ).then_inc(self.rstd_done.sem, 1)

    def act_norm(self, act, n, i):
        act.wait_ge(self.rstd_done.sem, self.rstd_done.count(n))
        act.wait_ge(self.xn_free.sem, self.xn_free.count(n - 2))
        x = columns(self.X, n, UNIT * C)
        for t in range(UNIT):
            self.nc.scalar.activation(self.xn[i][:, t], x[:, t * C:(t + 1) * C].unsqueeze(1).to_broadcast([P, 2, C]),
                                      ACT.Identity, scale=self.rstd[:, t:t + 1], bias=self.shift[:, t:t + 1]
                                      ).then_inc(self.xn_done.sem, 1)

    def pe_transpose(self, pe, n, i):
        pe.wait_ge(self.xn_done.sem, self.xn_done.count(n))
        pe.wait_ge(self.stack_done.sem, self.stack_done.count(n - 1))
        for t in range(UNIT):
            last = self.nc.tensor.transpose(self.xt_ps[:, t * P:(t + 1) * P],
                                            self.xn[i][:, t].rearrange("p a c -> p (a c)"), self.mem["ident"][:])
        last.then_inc(self.xt_done.sem, 1)

    def act_hi(self, act, n, i):
        act.wait_ge(self.xt_done.sem, self.xt_done.count(n))
        act.wait_ge(self.stack_free.sem, self.stack_free.count(n - 2))
        self.nc.scalar.activation(self.stack[i][:], self.xt_ps[:], ACT.Copy).then_inc(self.hi_done.sem, 1)

    def dve_lo(self, dve, n, i):
        dve.wait_ge(self.hi_done.sem, self.hi_done.count(n))
        self.nc.vector.tensor_tensor(self.stack[i][C:P], self.xt_ps[C:P], self.stack[i][C:P].bitcast(F32),
                                     ALU.subtract).then_inc(self.stack_done.sem, 1)


class Split:

    def __init__(self, ctx, nc, name, cols, pieces=1):
        self.nc, self.name, self.width = nc, name, cols // pieces
        self.hi, self.lo = (ctx.enter_context(nc.sbuf_tensor(f"{name}_{x}", [P, cols], F32R)) for x in ("hi", "lo"))
        buffers = range(min(pieces, 2))
        self.raw = [ctx.enter_context(nc.sbuf_tensor(f"{name}_raw{i}", [P, self.width], F32)) for i in buffers]
        self.loaded = [Signal(ctx, nc, f"{name}_loaded{i}", 16) for i in buffers]
        self.hi_done = Signal(ctx, nc, name + "_hi_done", 1)
        self.lo_done = Signal(ctx, nc, name + "_lo_done", 1)

    def load(self, sp, ins, n=0, i=0):
        sp.wait_ge(self.lo_done.sem, self.lo_done.count(n - 2))
        sp.dma_start(self.raw[i][:], columns(ins[self.name], n, self.width)).then_inc(self.loaded[i].sem, 16)

    def act_hi(self, act, n=0, i=0, q=0):
        act.wait_ge(self.loaded[i].sem, self.loaded[i].count(q))
        self.nc.scalar.activation(columns(self.hi, n, self.width), self.raw[i][:], ACT.Copy
                                  ).then_inc(self.hi_done.sem, 1)

    def dve_lo(self, dve, n=0, i=0):
        dve.wait_ge(self.hi_done.sem, self.hi_done.count(n))
        self.nc.vector.tensor_tensor(columns(self.lo, n, self.width), self.raw[i][:],
                                     columns(self.hi, n, self.width).bitcast(F32), ALU.subtract
                                     ).then_inc(self.lo_done.sem, 1)


class Moe:

    def __init__(self, ctx, nc, prefix, experts, chunks, hidden, guard):
        def sb(name, shape, dt=F32):
            return ctx.enter_context(nc.sbuf_tensor(prefix + name, shape, dt))

        self.nc, self.prefix, self.guard = nc, prefix, guard
        self.E, self.chunks, self.hidden = experts, chunks, hidden
        self.HALF = chunks * hidden
        self.LIST = 2 * TILES + experts
        self.REGION = TILES + 1
        self.FILL = 2 * P * TILES
        self.sent = nc.dram_tensor(prefix + "sent", ((experts * self.REGION + experts) * P, C + 2), F32).ap()
        self.done = nc.dram_tensor(prefix + "done", (self.FILL + 2 * experts * P, C), F32).ap()
        self.router = Split(ctx, nc, prefix + "router", experts)
        self.w_down = sb("w_down", [hidden, experts * chunks * C])
        self.router_bias = sb("router_bias", [P, experts])
        self.number = sb("number", [P, experts])
        self.region_row = sb("region_row", [P, experts])
        self.list_number = sb("list_number", [1, self.LIST])
        self.tile_of = sb("tile_of", [1, self.LIST], I32)
        self.expert_of = sb("expert_of", [1, self.LIST], I32)
        self.loaded = ctx.enter_context(nc.semaphore(prefix + "loaded"))
        self.loads = [(self.w_down, "w_down"), (self.router_bias, "router_bias"), (self.number, "number"),
                      (self.region_row, "region_row"), (self.list_number, "list_number")]
        self.w_up = Split(ctx, nc, prefix + "w_up", experts * 2 * self.HALF, UNITS)

    def load(self, sp, ins):
        self.router.load(sp, ins)
        for tile, name in self.loads:
            sp.dma_start(tile[:], ins[self.prefix + name]).then_inc(self.loaded, 16)
        sp.dma_start(self.sent[self.E * self.REGION * P:, :], ins[self.prefix + "fill"][self.E * P:, :]
                     ).then_inc(self.loaded, 16)

    def wait_loaded(self, eng):
        eng.wait_ge(self.loaded, 16 * (len(self.loads) + 1))


class Parts:
    pass


def routing(nc, ctx, mem, ins, X, moe, bank=None):
    prefix, E = moe.prefix, moe.E
    def sb(name, shape, dt=F32):
        return ctx.enter_context(nc.sbuf_tensor(prefix + name, shape, dt))

    used = []

    def sig(name, per=1):
        used.append(Signal(ctx, nc, prefix + name, per))
        return used[-1]

    def semaphore(name):
        return sig(name).sem

    front = Front(nc, ctx, mem, X, prefix, "eps5", bank)
    logit = sb("logit", [P, UNIT, E])
    top = sb("top", [P, UNIT, 8])
    top_at = sb("top_at", [P, UNIT, 8], U32)
    top_at_f = sb("top_at_f", [P, 2, UNIT])
    below, e_second = sb("below", [P, UNIT]), sb("e_second", [P, UNIT])
    shifted, e_all = sb("shifted", [P, UNIT, E]), sb("e_all", [P, UNIT, E])
    e_sum, denom = sb("e_sum", [P, UNIT]), sb("denom", [P, UNIT])
    chosen = sb("chosen", [P, 2, UNIT, E])
    both = [sb(f"both{i}", [P, UNIT + 1, E], BF16) for i in range(2)]
    place = sb("place", [P, UNIT, E])
    slot_f = sb("slot_f", [P, 2, UNIT])
    slot = [sb(f"slot{i}", [P, 2, UNIT], U32) for i in range(2)]
    rows = [sb(f"rows{i}", [P, UNIT, 2, C + 2]) for i in range(2)]
    before, ones = sb("before", [P, P], BF16), sb("ones", [P, P], BF16)
    before_f = sb("before_f", [P, P])
    done_row = sb("done_row", [P, TILES * 2])
    fill = sb("fill", [P, E, C + 2])
    threshold = sb("threshold", [P, TILES])
    router_ps, rank_ps = (bank or ctx.enter_context(nc.psum_tensor(prefix + x, [P, 512], F32))
                          for x in ("router_ps", "rank_ps"))

    spare = sig("spare")
    loaded = semaphore("route_loaded")
    made = semaphore("made")
    logits_done = sig("logits_done")
    logit_kept = sig("logit_kept")
    top_done = sig("top_done", 2 * UNIT + 1)
    gate_a = sig("gate_a", 2)
    gate_e = sig("gate_e", 2)
    gate_b = sig("gate_b", 5)
    chosen_done = sig("chosen_done", 2)
    both_done = sig("both_done", 2)
    ranked = sig("ranked")
    placed = sig("placed", 3)
    slots_done = sig("slots_done")
    rows_done = sig("rows_done", 2)
    sent = mem["sent"]
    front.stack_free = logits_done
    front.xn_free = rows_done

    LOADS = [(before_f, ins["before"]), (done_row, ins["done_row"]), (threshold, ins["threshold"]),
             (fill, ins[prefix + "fill"][0:E * P, :].rearrange("(e p) c -> p e c", p=P))]

    def pe_logits(pe, n, i):
        pe.wait_ge(front.stack_done.sem, front.stack_done.count(n))
        pe.wait_ge(logit_kept.sem, logit_kept.count(n - 1))
        for t in range(UNIT):
            tokens = front.stack[i][:, t * P:(t + 1) * P]
            nc.tensor.matmul(router_ps[:, t * E:(t + 1) * E], tokens, moe.router.lo[:], start=True, stop=False)
            last = nc.tensor.matmul(router_ps[:, t * E:(t + 1) * E], tokens, moe.router.hi[:],
                                    start=False, stop=True)
        last.then_inc(logits_done.sem, 1)

    def dve_logits(dve, n):
        dve.wait_ge(logits_done.sem, logits_done.count(n))
        nc.vector.tensor_tensor(logit[:], router_ps[:, 0:UNIT * E].rearrange("p (t e) -> p t e", t=UNIT),
                                moe.router_bias[:].unsqueeze(1).to_broadcast([P, UNIT, E]), ALU.add
                                ).then_inc(logit_kept.sem, 1)

    def dve_top(dve, n):
        dve.wait_ge(logit_kept.sem, logit_kept.count(n))
        stand_alone(dve, spare)
        for t in range(UNIT):
            nc.vector.max(top[:, t], logit[:, t]).then_inc(top_done.sem, 1)
        dve.wait_ge(top_done.sem, top_done.count(n, UNIT))
        stand_alone(dve, spare)
        for t in range(UNIT):
            nc.vector.max_index(top_at[:, t], top[:, t], logit[:, t]).then_inc(top_done.sem, 1)
        nc.vector.tensor_tensor(below[:], top[:, :, 1], top[:, :, 0], ALU.subtract).then_inc(gate_a.sem, 1)
        nc.vector.tensor_tensor(shifted[:], logit[:], top[:, :, 0:1].to_broadcast([P, UNIT, E]),
                                ALU.subtract).then_inc(gate_a.sem, 1)
        dve.wait_ge(top_done.sem, top_done.count(n, 2 * UNIT))
        nc.vector.tensor_copy(top_at_f[:].rearrange("p k t -> p t k"), top_at[:, :, 0:2]
                              ).then_inc(top_done.sem, 1)

    def dve_choose(dve, n, i):
        dve.wait_ge(top_done.sem, top_done.count(n))
        for k in range(2):
            nc.vector.tensor_tensor(chosen[:, k], moe.number[:].unsqueeze(1).to_broadcast([P, UNIT, E]),
                                    top_at_f[:, k].unsqueeze(2).to_broadcast([P, UNIT, E]), ALU.is_equal
                                    ).then_inc(chosen_done.sem, 1)
        dve.wait_ge(chosen_done.sem, chosen_done.count(n))
        nc.vector.tensor_tensor(both[i][:, 0:UNIT], chosen[:, 0], chosen[:, 1], ALU.add
                                ).then_inc(both_done.sem, 1)
        dve.wait_ge(both_done.sem, both_done.count(n, 1))
        dve.wait_ge(ranked.sem, ranked.count(n - 1))
        with nc.allow_low_precision(reason="counts up to 64, exact in bfloat16"):
            nc.vector.tensor_reduce(both[1 - i][:, UNIT], both[i][:].rearrange("p t e -> p e t"), axis=AX.X,
                                    op=ALU.add).then_inc(both_done.sem, 1)

    def pe_rank(pe, n, i):
        pe.wait_ge(both_done.sem, both_done.count(n, 1))
        pe.wait_ge(placed.sem, placed.count(n - 1, 1))
        flat = both[i][:].rearrange("p t e -> p (t e)")
        nc.tensor.matmul(rank_ps[:, 0:UNIT * E], before[:], flat[:, 0:UNIT * E], start=True, stop=False,
                         skip_group_check=True)
        for t in range(UNIT - 1):
            for later in range(t + 1, UNIT):
                nc.tensor.matmul(rank_ps[:, later * E:(later + 1) * E], ones[:], both[i][:, t],
                                 start=False, stop=False, skip_group_check=True)
        for t in range(UNIT):
            last = nc.tensor.matmul(rank_ps[:, t * E:(t + 1) * E], ones[:], both[i][:, UNIT],
                                    start=False, stop=True, skip_group_check=True)
        last.then_inc(ranked.sem, 1)

    def act_gate(act, n):
        act.wait_ge(gate_a.sem, gate_a.count(n))
        nc.scalar.activation(e_second[:], below[:], ACT.Exp).then_inc(gate_e.sem, 1)
        nc.scalar.activation(e_all[:], shifted[:], ACT.Exp).then_inc(gate_e.sem, 1)

    def dve_room(dve, i, q):
        if not isinstance(q, int) or q > 0:
            dve.wait_ge(sent[i].sem, sent[i].count(q - 1))

    def dve_rows(dve, n, i):
        dve.wait_ge(front.xt_done.sem, front.xt_done.count(n))
        nc.vector.tensor_copy(rows[i][:, :, :, 0:C], front.xn[i][:, :, 0:1].to_broadcast([P, UNIT, 2, C])
                              ).then_inc(rows_done.sem, 1)
        nc.vector.tensor_copy(rows[i][:, :, :, C], columns(done_row, n, 2 * UNIT).rearrange("p (t k) -> p t k", k=2)
                              ).then_inc(rows_done.sem, 1)

    def dve_gate(dve, n, i):
        dve.wait_ge(gate_e.sem, gate_e.count(n))
        nc.vector.tensor_reduce(e_sum[:], e_all[:], axis=AX.X, op=ALU.add).then_inc(gate_b.sem, 1)
        dve.wait_ge(gate_b.sem, gate_b.count(n, 1))
        nc.vector.tensor_scalar(denom[:], e_sum[:], moe.guard, 1.0, ALU.mult, ALU.add).then_inc(gate_b.sem, 1)
        dve.wait_ge(gate_b.sem, gate_b.count(n, 2))
        nc.vector.tensor_tensor(denom[:], denom[:], e_second[:], ALU.add).then_inc(gate_b.sem, 1)
        dve.wait_ge(gate_b.sem, gate_b.count(n, 3))
        nc.vector.reciprocal(rows[i][:, :, 0, C + 1], denom[:]).then_inc(gate_b.sem, 1)
        dve.wait_ge(gate_b.sem, gate_b.count(n, 4))
        nc.vector.tensor_tensor(rows[i][:, :, 1, C + 1], rows[i][:, :, 0, C + 1], e_second[:], ALU.mult
                                ).then_inc(gate_b.sem, 1)

    def dve_slots(dve, n, i):
        dve.wait_ge(ranked.sem, ranked.count(n))
        nc.vector.tensor_tensor(place[:], rank_ps[:, 0:UNIT * E].rearrange("p (t e) -> p t e", t=UNIT),
                                moe.region_row[:].unsqueeze(1).to_broadcast([P, UNIT, E]), ALU.add
                                ).then_inc(placed.sem, 1)
        dve.wait_ge(placed.sem, placed.count(n, 1))
        nc.vector.tensor_tensor(chosen[:], chosen[:], place[:].unsqueeze(1).to_broadcast([P, 2, UNIT, E]),
                                ALU.mult).then_inc(placed.sem, 1)
        dve.wait_ge(placed.sem, placed.count(n, 2))
        nc.vector.tensor_reduce(slot_f[:], chosen[:], axis=AX.X, op=ALU.add).then_inc(placed.sem, 1)
        dve.wait_ge(placed.sem, placed.count(n))
        nc.vector.tensor_copy(slot[i][:], slot_f[:]).then_inc(slots_done.sem, 1)

    def dve_slots_gate(dve, n, i):
        dve.wait_ge(ranked.sem, ranked.count(n))
        nc.vector.tensor_tensor(place[:], rank_ps[:, 0:UNIT * E].rearrange("p (t e) -> p t e", t=UNIT),
                                moe.region_row[:].unsqueeze(1).to_broadcast([P, UNIT, E]), ALU.add
                                ).then_inc(placed.sem, 1)
        dve.wait_ge(gate_e.sem, gate_e.count(n))
        nc.vector.tensor_reduce(e_sum[:], e_all[:], axis=AX.X, op=ALU.add).then_inc(gate_b.sem, 1)
        dve.wait_ge(placed.sem, placed.count(n, 1))
        nc.vector.tensor_tensor(chosen[:], chosen[:], place[:].unsqueeze(1).to_broadcast([P, 2, UNIT, E]),
                                ALU.mult).then_inc(placed.sem, 1)
        dve.wait_ge(gate_b.sem, gate_b.count(n, 1))
        nc.vector.tensor_scalar(denom[:], e_sum[:], moe.guard, 1.0, ALU.mult, ALU.add).then_inc(gate_b.sem, 1)
        dve.wait_ge(placed.sem, placed.count(n, 2))
        nc.vector.tensor_reduce(slot_f[:], chosen[:], axis=AX.X, op=ALU.add).then_inc(placed.sem, 1)
        dve.wait_ge(gate_b.sem, gate_b.count(n, 2))
        nc.vector.tensor_tensor(denom[:], denom[:], e_second[:], ALU.add).then_inc(gate_b.sem, 1)
        dve.wait_ge(placed.sem, placed.count(n))
        nc.vector.tensor_copy(slot[i][:], slot_f[:]).then_inc(slots_done.sem, 1)
        dve.wait_ge(gate_b.sem, gate_b.count(n, 3))
        nc.vector.reciprocal(rows[i][:, :, 0, C + 1], denom[:]).then_inc(gate_b.sem, 1)
        dve.wait_ge(gate_b.sem, gate_b.count(n, 4))
        nc.vector.tensor_tensor(rows[i][:, :, 1, C + 1], rows[i][:, :, 0, C + 1], e_second[:], ALU.mult
                                ).then_inc(gate_b.sem, 1)

    def pool_send(pool, n, i, tiles=range(UNIT)):
        if 0 in tiles:
            pool.wait_ge(slots_done.sem, slots_done.count(n))
            pool.wait_ge(rows_done.sem, rows_done.count(n))
            pool.wait_ge(gate_b.sem, gate_b.count(n))
            stand_alone(pool, spare)
        for t in tiles:
            for k in range(2):
                nc.gpsimd.indirect_dma_start(
                    out=moe.sent, out_offset=bass.IndirectOffsetOnAxis(ap=slot[i][:, k, t:t + 1], axis=0),
                    in_=rows[i][:, t, k], in_offset=None).then_inc(sent[i].sem, 16)

    def prepare():
        with nc.Block() as block:
            @block.sync
            def _(sp):
                for tile, src in LOADS:
                    sp.dma_start(tile[:], src).then_inc(loaded, 16)

            @block.gpsimd
            def _(pool):
                nc.gpsimd.memset(ones[:], 1.0)

            @block.scalar
            def _(act):
                moe.router.act_hi(act)

            @block.vector
            def _(dve):
                for i in range(2):
                    nc.vector.memset(both[i][:, UNIT], 0.0)
                moe.router.dve_lo(dve)
                moe.wait_loaded(dve)
                dve.wait_ge(loaded, 16 * len(LOADS))
                nc.vector.tensor_copy(before[:], before_f[:])

    def finish():
        with ExitStack() as ctx:
            def sb(name, shape, dt=F32):
                return ctx.enter_context(nc.sbuf_tensor(prefix + name, shape, dt))

            count = sb("count", [P, E])
            fill_f, fill_row = sb("fill_f", [P, E]), sb("fill_row", [P, E], U32)
            over = sb("over", [1, E, TILES])
            tiles_of, tiles_upto, skip, one = (sb(x, [1, E]) for x in ("tiles_of", "tiles_upto", "skip", "one"))
            behind = sb("behind", [1, moe.LIST, E])
            jump = sb("jump", [1, moe.LIST, E])
            tile_f, expert_f = sb("tile_f", [1, moe.LIST]), sb("expert_f", [1, moe.LIST])
            step, fill_at = semaphore("step"), semaphore("fill_at")
            counted = semaphore("counted")
            with nc.Block() as block:
                @block.tensor
                def _(pe):
                    nc.tensor.matmul(rank_ps[:, 0:E], ones[:], both[UNITS % 2][:, UNIT], start=True, stop=True
                                     ).then_inc(counted, 1)

                @block.vector
                def _(dve):
                    done = [0]

                    def counts(ins):
                        done[0] += 1
                        ins.then_inc(step, 1)

                    dve.wait_ge(counted, 1)
                    counts(nc.vector.tensor_copy(count[:], rank_ps[:, 0:E]))
                    counts(nc.vector.memset(one[:], 1.0))
                    dve.wait_ge(step, done[0])
                    counts(nc.vector.tensor_tensor(fill_f[:], count[:], moe.region_row[:], ALU.add))
                    dve.wait_ge(step, done[0])
                    counts(nc.vector.tensor_scalar(fill_f[:], fill_f[:], fill[:, 0, C:C + 1], -float(moe.FILL),
                                                   ALU.add, ALU.add))
                    dve.wait_ge(step, done[0])
                    nc.vector.tensor_copy(fill_row[:], fill_f[:]).then_inc(fill_at, 1)
                    counts(nc.vector.tensor_tensor(over[:], count[0:1].unsqueeze(2).to_broadcast([1, E, TILES]),
                                                   threshold[0:1].unsqueeze(1).to_broadcast([1, E, TILES]), ALU.is_gt))
                    dve.wait_ge(step, done[0])
                    counts(nc.vector.tensor_reduce(tiles_of[:], over[:], axis=AX.X, op=ALU.add))
                    dve.wait_ge(step, done[0])
                    counts(nc.vector.tensor_tensor_scan(tiles_upto[:], one[:], tiles_of[:], 0.0, ALU.mult, ALU.add))
                    counts(nc.vector.tensor_scalar(skip[:], tiles_of[:], -1.0, float(moe.REGION), ALU.mult, ALU.add))
                    dve.wait_ge(step, done[0])
                    counts(nc.vector.tensor_tensor(
                        behind[:], moe.list_number[:].unsqueeze(2).to_broadcast([1, moe.LIST, E]),
                        tiles_upto[:].unsqueeze(1).to_broadcast([1, moe.LIST, E]), ALU.is_ge))
                    dve.wait_ge(step, done[0])
                    counts(nc.vector.tensor_tensor(jump[:], behind[:], skip[:].unsqueeze(1).to_broadcast([1, moe.LIST, E]),
                                                   ALU.mult))
                    counts(nc.vector.tensor_reduce(expert_f[:], behind[:, :, 0:E - 1], axis=AX.X, op=ALU.add))
                    dve.wait_ge(step, done[0])
                    counts(nc.vector.tensor_reduce(tile_f[:], jump[:], axis=AX.X, op=ALU.add))
                    counts(nc.vector.tensor_copy(moe.expert_of[:], expert_f[:]))
                    dve.wait_ge(step, done[0])
                    counts(nc.vector.tensor_tensor(tile_f[:], tile_f[:], moe.list_number[:], ALU.add))
                    dve.wait_ge(step, done[0])
                    nc.vector.tensor_copy(moe.tile_of[:], tile_f[:])

                @block.gpsimd
                def _(pool):
                    pool.wait_ge(fill_at, 1)
                    for e in range(E):
                        nc.gpsimd.indirect_dma_start(
                            out=moe.sent, out_offset=bass.IndirectOffsetOnAxis(ap=fill_row[:, e:e + 1], axis=0),
                            in_=fill[:, e], in_offset=None).then_inc(mem["filled"].sem, 16)
                    pool.wait_ge(mem["filled"].sem, mem["filled"].count(E - 1))
                    for i in range(2):
                        pool.wait_ge(sent[i].sem, sent[i].count(UNITS // 2 - 1))
            clear(nc, used + front.used)
            for signal in sent:
                signal.start_over(UNITS // 2)
            mem["filled"].start_over(E)

    parts = Parts()
    parts.front = front
    parts.prepare = prepare
    parts.finish = finish
    parts.pe_logits = pe_logits
    parts.pe_rank = pe_rank
    parts.act_gate = act_gate
    parts.dve_logits = dve_logits
    parts.dve_top = dve_top
    parts.dve_room = dve_room
    parts.logit_kept = logit_kept
    parts.placed = placed
    parts.dve_choose = dve_choose
    parts.dve_rows = dve_rows
    parts.dve_slots = dve_slots
    parts.dve_gate = dve_gate
    parts.dve_slots_gate = dve_slots_gate
    parts.pool_send = pool_send
    return parts


def experts_phase(nc, mem, X, moe, out=None, stored=None):
    prefix, E, chunks, hidden, HALF, LIST = moe.prefix, moe.E, moe.chunks, moe.hidden, moe.HALF, moe.LIST
    BANKS = -(-HALF // 512)
    SEG = HALF // BANKS
    TOGETHER = 2 * HALF <= 512
    DEPTH = 2 if TOGETHER else 1
    HT_BANKS = -(-chunks * P // 512)
    with ExitStack() as ctx:
        def sb(name, shape, dt=F32):
            return ctx.enter_context(nc.sbuf_tensor(prefix + name, shape, dt))

        def ps(name, banks=1):
            return ctx.enter_context(nc.psum_tensor(prefix + name, [P, banks, 512], F32))

        used = []

        def sig(name, per=1):
            used.append(Signal(ctx, nc, prefix + name, per))
            return used[-1]

        x_in = [sb(f"x_in{i}", [P, 2 * C + 2]) for i in range(PASS)]
        done_at = [sb(f"done_at{i}", [P, 1], U32) for i in range(PASS)]
        gate = [sb(f"gate{i}", [P, 1]) for i in range(PASS)]
        stack = [sb(f"x_stack{i}", [P, P], F32R) for i in range(2)]
        silu = [sb(f"silu{d}", [P, BANKS, SEG]) for d in range(DEPTH)]
        h_sb = [sb(f"h_sb{d}", [P, BANKS, SEG]) for d in range(DEPTH)]
        ht_sb = [sb(f"ht_sb{i}", [hidden, chunks * P]) for i in range(2)]
        y_sb = [sb(f"y_sb{i}", [P, C]) for i in range(PASS)]
        xt_ps = ps("x_t_ps")
        y_ps = [ps(f"y_ps{d}") for d in range(DEPTH)]
        if TOGETHER:
            h12_ps = [ps(f"h12_ps{d}") for d in range(DEPTH)]
            h1 = [h12_ps[d][:, :, 0:SEG] for d in range(DEPTH)]
            h2 = [h12_ps[d][:, :, SEG:2 * SEG] for d in range(DEPTH)]
        else:
            h1_ps, h2_ps = ps("h1_ps", BANKS), ps("h2_ps", BANKS)
            h1, h2 = [h1_ps[:, :, 0:SEG]], [h2_ps[:, :, 0:SEG]]
        ht_ps = [ps(f"ht_ps{d}", HT_BANKS) for d in range(DEPTH)]

        spare = sig("x_spare")
        x_loaded = [sig(f"x_loaded{i}", 32) for i in range(PASS)]
        xt_done = sig("x_t_done")
        hi_kept = sig("hi_kept")
        stack_done = sig("x_stack_done")
        h1_done, h2_done = sig("h1_done"), sig("h2_done")
        silu_done = sig("silu_done")
        h_kept = sig("h_kept")
        ht_done = sig("ht_done")
        ht_kept = sig("ht_kept")
        y_done = sig("y_done")
        ends_kept = sig("ends_kept", 2)
        y_kept = sig("y_kept")
        y_sent = mem["y_sent"]

        def load_x(sp, n, q, i):
            sp.wait_ge(xt_done.sem, xt_done.count(n - PASS))
            sp.wait_ge(ends_kept.sem, ends_kept.count(n - PASS))
            tile = sp.value_load(moe.tile_of[0:1, bass.ds(n, 1)], min_val=0, max_val=E * moe.REGION + E - 1)
            rows = moe.sent[bass.ds(tile * P, P), :]
            sp.dma_start(x_in[i][:, 0:C], rows[:, 0:C]).then_inc(x_loaded[i].sem, 16)
            sp.dma_start(x_in[i][:, C:], rows).then_inc(x_loaded[i].sem, 16)

        def pool_ends(pool, n, q, i):
            pool.wait_ge(x_loaded[i].sem, x_loaded[i].count(q))
            pool.wait_ge(y_kept.sem, y_kept.count(n - PASS))
            if not isinstance(q, int) or q > 0:
                pool.wait_ge(y_sent[i].sem, y_sent[i].count(q - 1))
            stand_alone(pool, spare)
            nc.gpsimd.tensor_copy(done_at[i][:], x_in[i][:, 2 * C:2 * C + 1]).then_inc(ends_kept.sem, 1)
            nc.gpsimd.tensor_copy(gate[i][:], x_in[i][:, 2 * C + 1:2 * C + 2]).then_inc(ends_kept.sem, 1)

        def pool_send(pool, n, q, i):
            pool.wait_ge(y_kept.sem, y_kept.count(n))
            pool.wait_ge(ends_kept.sem, ends_kept.count(n))
            stand_alone(pool, spare)
            nc.gpsimd.indirect_dma_start(
                out=moe.done, out_offset=bass.IndirectOffsetOnAxis(ap=done_at[i][:, 0:1], axis=0),
                in_=y_sb[i][:], in_offset=None).then_inc(y_sent[i].sem, 16)

        def pe_transpose(pe, n, q, i):
            pe.wait_ge(x_loaded[i].sem, x_loaded[i].count(q))
            pe.wait_ge(stack_done.sem, stack_done.count(n - 1))
            nc.tensor.transpose(xt_ps[:, 0, 0:P], x_in[i][:, 0:2 * C], mem["ident"][:]).then_inc(xt_done.sem, 1)

        def expert_of_tile(n):
            return nc.tensor.value_load(moe.expert_of[0:1, bass.ds(n, 1)], min_val=0, max_val=E - 1)

        def pe_up(pe, n, i, e):
            pe.wait_ge(stack_done.sem, stack_done.count(n))
            pe.wait_ge(h_kept.sem, h_kept.count(n - DEPTH))
            if TOGETHER:
                for w in (moe.w_up.lo, moe.w_up.hi):
                    last = nc.tensor.matmul(h12_ps[i % 2][:, 0, 0:2 * HALF], stack[i % 2][:],
                                            w[:, bass.ds(e * (2 * HALF), 2 * HALF)],
                                            start=w is moe.w_up.lo, stop=w is moe.w_up.hi)
                last.then_inc(h1_done.sem, 1)
                return
            for m, (bank, done) in enumerate(((h1_ps, h1_done), (h2_ps, h2_done))):
                for b in range(BANKS):
                    for w in (moe.w_up.lo, moe.w_up.hi):
                        last = nc.tensor.matmul(bank[:, b, 0:SEG], stack[i % 2][:],
                                                w[:, bass.ds(e * (2 * HALF) + (m * HALF + b * SEG), SEG)],
                                                start=w is moe.w_up.lo, stop=w is moe.w_up.hi)
                last.then_inc(done.sem, 1)

        def pe_transpose_h(pe, n, i):
            pe.wait_ge(h_kept.sem, h_kept.count(n))
            pe.wait_ge(ht_kept.sem, ht_kept.count(n - DEPTH))
            flat = h_sb[i % DEPTH][:].rearrange("p b s -> p (b s)")
            for c in range(chunks):
                b, at = divmod(c * P, 512)
                last = nc.tensor.transpose(ht_ps[i % DEPTH][0:hidden, b, at:at + P],
                                           flat[:, c * hidden:(c + 1) * hidden], mem["ident"][:])
            last.then_inc(ht_done.sem, 1)

        def pe_down(pe, n, i, e):
            pe.wait_ge(ht_kept.sem, ht_kept.count(n))
            pe.wait_ge(y_kept.sem, y_kept.count(n - DEPTH))
            for c in range(chunks):
                last = nc.tensor.matmul(y_ps[i % DEPTH][:, 0, 0:C], ht_sb[i % 2][:, c * P:(c + 1) * P],
                                        moe.w_down[:, bass.ds(e * (chunks * C) + c * C, C)],
                                        start=c == 0, stop=c == chunks - 1)
            last.then_inc(y_done.sem, 1)

        def act_hi(act, n, i):
            act.wait_ge(xt_done.sem, xt_done.count(n))
            act.wait_ge(h_last.sem, h_last.count(n - 2))
            nc.scalar.activation(stack[i % 2][:], xt_ps[:, 0, 0:P], ACT.Copy).then_inc(hi_kept.sem, 1)

        def dve_lo(dve, n, i):
            dve.wait_ge(hi_kept.sem, hi_kept.count(n))
            nc.vector.tensor_tensor(stack[i % 2][C:P], xt_ps[C:P, 0, 0:P], stack[i % 2][C:P].bitcast(F32),
                                    ALU.subtract).then_inc(stack_done.sem, 1)

        h_last = h1_done if TOGETHER else h2_done

        def act_silu(act, n, i):
            act.wait_ge(h1_done.sem, h1_done.count(n))
            act.wait_ge(h_kept.sem, h_kept.count(n - DEPTH))
            nc.scalar.activation(silu[i % DEPTH][:], h1[i % DEPTH], ACT.Silu).then_inc(silu_done.sem, 1)

        def dve_hidden(dve, n, i):
            dve.wait_ge(h_last.sem, h_last.count(n))
            dve.wait_ge(ht_done.sem, ht_done.count(n - DEPTH))
            dve.wait_ge(silu_done.sem, silu_done.count(n))
            nc.vector.tensor_tensor(h_sb[i % DEPTH][:], h2[i % DEPTH], silu[i % DEPTH][:], ALU.mult
                                    ).then_inc(h_kept.sem, 1)

        def act_keep_ht(act, n, i):
            act.wait_ge(ht_done.sem, ht_done.count(n))
            act.wait_ge(y_done.sem, y_done.count(n - 2))
            nc.scalar.activation(ht_sb[i % 2][:],
                                 ht_ps[i % DEPTH][0:hidden].rearrange("p b c -> p (b c)")[:, 0:chunks * P],
                                 ACT.Copy).then_inc(ht_kept.sem, 1)

        def dve_keep_y(dve, n, q, i):
            dve.wait_ge(y_done.sem, y_done.count(n))
            dve.wait_ge(ends_kept.sem, ends_kept.count(n))
            if not isinstance(q, int) or q > 0:
                dve.wait_ge(y_sent[i].sem, y_sent[i].count(q - 1))
            nc.vector.tensor_scalar(y_sb[i][:], y_ps[i % DEPTH][:, 0, 0:C], gate[i][:, 0:1], None, ALU.mult
                                    ).then_inc(y_kept.sem, 1)

        def at_step(q, i, by):
            q, i = q + (i + by) // PASS, (i + by) % PASS
            n = PASS * q + i
            return None if isinstance(n, int) and not 0 <= n < LIST else (n, q, i)

        def pe_step(pe, q, i, experts):
            if at := at_step(q, i, 0):
                experts.append(expert_of_tile(at[0]))
                pe_up(pe, at[0], at[2], experts[i])
            if at := at_step(q, i, -1):
                pe_transpose_h(pe, at[0], at[2])
            if at := at_step(q, i, 2):
                pe_transpose(pe, *at)
            if at := at_step(q, i, -2):
                pe_down(pe, at[0], at[2], experts[i - 2] if i >= 2 else expert_of_tile(at[0]))

        def act_step(act, q, i):
            if at := at_step(q, i, 0):
                act_silu(act, at[0], at[2])
            if at := at_step(q, i, -1):
                act_keep_ht(act, at[0], at[2])
            if at := at_step(q, i, 2):
                act_hi(act, at[0], at[2])

        def dve_step(dve, q, i):
            if at := at_step(q, i, -3):
                dve_keep_y(dve, *at)
            if at := at_step(q, i, 0):
                dve_hidden(dve, at[0], at[2])
            if at := at_step(q, i, 2):
                dve_lo(dve, at[0], at[2])

        def pool_step(pool, q, i):
            if at := at_step(q, i, 2):
                pool_ends(pool, *at)
            if at := at_step(q, i, -3):
                pool_send(pool, *at)

        PASSES = LIST // PASS
        with nc.Block() as block:
            @block.sync
            def _(sp):
                for i in range(PASS):
                    load_x(sp, i, 0, i)
                with nc.sync.Fori(1, PASSES) as q:
                    for i in range(PASS):
                        load_x(sp, PASS * q + i, q, i)

            @block.tensor
            def _(pe):
                for i in range(2):
                    pe_transpose(pe, i, 0, i)
                experts = []
                for i in range(PASS):
                    pe_step(pe, 0, i, experts)
                with nc.tensor.Fori(1, PASSES - 1) as q:
                    experts = []
                    for i in range(PASS):
                        pe_step(pe, q, i, experts)
                experts = []
                for i in range(PASS + 2):
                    pe_step(pe, PASSES - 1, i, experts)

            @block.scalar
            def _(act):
                for i in range(2):
                    act_hi(act, i, i)
                for i in range(PASS):
                    act_step(act, 0, i)
                with nc.scalar.Fori(1, PASSES - 1) as q:
                    for i in range(PASS):
                        act_step(act, q, i)
                for i in range(PASS + 3):
                    act_step(act, PASSES - 1, i)

            @block.vector
            def _(dve):
                for i in range(2):
                    dve_lo(dve, i, i)
                for i in range(PASS):
                    dve_step(dve, 0, i)
                with nc.vector.Fori(1, PASSES - 1) as q:
                    for i in range(PASS):
                        dve_step(dve, q, i)
                for i in range(PASS + 3):
                    dve_step(dve, PASSES - 1, i)

            @block.gpsimd
            def _(pool):
                for i in range(2):
                    pool_ends(pool, i, 0, i)
                for i in range(PASS):
                    pool_step(pool, 0, i)
                with nc.gpsimd.Fori(1, PASSES - 1) as q:
                    for i in range(PASS):
                        pool_step(pool, q, i)
                for i in range(PASS + 3):
                    pool_step(pool, PASSES - 1, i)
                for i in range(PASS):
                    pool.wait_ge(y_sent[i].sem, y_sent[i].count(PASSES - 1))
        clear(nc, used)
        for signal in y_sent:
            signal.start_over(PASSES)

    PARTS = 8
    WIDTH = TILES * C // PARTS
    with ExitStack() as ctx:
        back = ctx.enter_context(nc.sbuf_tensor(prefix + "back", [P, 2, TILES * C], F32))
        back_in = [ctx.enter_context(nc.semaphore(f"{prefix}back_in{part}")) for part in range(PARTS)]
        added = ctx.enter_context(nc.semaphore(prefix + "added"))
        with nc.Block() as block:
            @block.sync
            def _(sp):
                for part in range(PARTS):
                    for k in range(2):
                        rows = moe.done[k * P * TILES:(k + 1) * P * TILES, :].rearrange("(p t) c -> p (t c)", t=TILES)
                        cols = slice(part * WIDTH, (part + 1) * WIDTH)
                        sp.dma_start(back[:, k, cols], rows[:, cols]).then_inc(back_in[part], 16)
                if out is not None:
                    for part in range(PARTS):
                        sp.wait_ge(added, 2 * part + 2)
                        cols = slice(part * WIDTH, (part + 1) * WIDTH)
                        sp.dma_start(out[:, cols], X[:, cols]).then_inc(stored, 16)
                    sp.wait_ge(stored, 16 * PARTS)

            @block.vector
            def _(dve):
                for part in range(PARTS):
                    cols = slice(part * WIDTH, (part + 1) * WIDTH)
                    dve.wait_ge(back_in[part], 32)
                    nc.vector.tensor_tensor(X[:, cols], X[:, cols], back[:, 0, cols], ALU.add).then_inc(added, 1)
                    dve.wait_ge(added, 2 * part + 1)
                    nc.vector.tensor_tensor(X[:, cols], X[:, cols], back[:, 1, cols], ALU.add).then_inc(added, 1)


def mixing_phase(nc, mem, ins, X, moe):
    with ExitStack() as route_ctx:
        route = routing(nc, route_ctx, mem, ins, X, moe)
        mix(nc, mem, ins, X, moe, route)
        route.finish()


def mix(nc, mem, ins, X, moe, route):
    with ExitStack() as ctx:
        def sb(name, shape, dt=F32):
            return ctx.enter_context(nc.sbuf_tensor("mx_" + name, shape, dt))

        def pb(name):
            return ctx.enter_context(nc.psum_tensor("mx_" + name, [P, 512], F32))

        used = []

        def sig(name, per=1):
            used.append(Signal(ctx, nc, "mx_" + name, per))
            return used[-1]

        N = 2 * P
        front = Front(nc, ctx, mem, X, "mx_", "eps6")
        w = Split(ctx, nc, "mx_w", 2 * P + 2)
        b = sb("b", [P, 3])
        loaded = sig("loaded")
        with nc.Block() as block:
            @block.sync
            def _(sp):
                sp.dma_start(b[:], ins["mx_b"]).then_inc(loaded.sem, 16)
                w.load(sp, ins)
                moe.load(sp, ins)
                sp.wait_ge(loaded.sem, 16)

            @block.scalar
            def _(act):
                w.act_hi(act)

            @block.vector
            def _(dve):
                w.dve_lo(dve)

        x0, x2 = [sb(f"x0{i}", [P, 2, N]) for i in range(2)], [sb(f"x2{i}", [P, 2, N]) for i in range(2)]
        x1 = sb("x1", [P, 2, 2])
        most, least = sb("most", [P, 2]), sb("least", [P, 2])
        by_most, by_least = sb("by_most", [P, 2, 2]), sb("by_least", [P, 2, 2])
        bias = sb("bias", [P, 2, 2])
        weight = [sb(f"weight{i}", [P, N]) for i in range(2)]
        product = [sb(f"product{i}", [P, N]) for i in range(2)]
        den, num, feats = sb("den", [P, UNIT]), sb("num", [P, UNIT]), sb("feats", [P, UNIT])
        e_minus, gate = sb("e_minus", [P, UNIT]), sb("gate", [P, UNIT])
        x0_ps, x2_ps, x1_ps = pb("x0_ps"), pb("x2_ps"), pb("x1_ps")

        spare = sig("spare", 0)
        up_done = sig("up_done", 3)
        x0_kept = sig("x0_kept")
        x2_kept = sig("x2_kept")
        x1_kept = sig("x1_kept")
        bound = sig("bound", 6)
        weighted = sig("weighted", UNIT)
        summed = sig("summed", UNIT)
        feats_done = sig("feats_done", 2)
        e_done = sig("e_done")
        gate_done = sig("gate_done", 2)
        x_added = sig("x_added", UNIT)
        front.stack_free = up_done
        front.xn_free = x_added

        def pe_up(pe, n, i):
            pe.wait_ge(front.stack_done.sem, front.stack_done.count(n))
            pe.wait_ge(x2_kept.sem, x2_kept.count(n - 1))
            pe.wait_ge(x0_kept.sem, x0_kept.count(n - 1))
            pe.wait_ge(x1_kept.sem, x1_kept.count(n - 1))
            for k, bank in enumerate((x0_ps, x2_ps)):
                cols = slice(k * P, (k + 1) * P)
                nc.tensor.matmul(bank[:], w.lo[:, cols], front.stack[i][:], start=True, stop=False)
                nc.tensor.matmul(bank[:], w.hi[:, cols], front.stack[i][:], start=False, stop=True
                                 ).then_inc(up_done.sem, 1)
            for t in range(UNIT):
                tokens = front.stack[i][:, t * P:(t + 1) * P]
                nc.tensor.matmul(x1_ps[:, 2 * t:2 * t + 2], tokens, w.lo[:, 2 * P:], start=True, stop=False)
                last = nc.tensor.matmul(x1_ps[:, 2 * t:2 * t + 2], tokens, w.hi[:, 2 * P:], start=False, stop=True)
            last.then_inc(up_done.sem, 1)

        def act_keep(act, n, i):
            act.wait_ge(up_done.sem, up_done.count(n, 1))
            act.wait_ge(weighted.sem, weighted.count(n - 1))
            nc.scalar.activation(x0[i][:].rearrange("p m n -> p (m n)"), x0_ps[:], ACT.Identity,
                                 bias=b[:, 0:1]).then_inc(x0_kept.sem, 1)
            act.wait_ge(up_done.sem, up_done.count(n, 2))
            act.wait_ge(summed.sem, summed.count(n - 2))
            nc.scalar.activation(x2[i][:].rearrange("p m n -> p (m n)"), x2_ps[:], ACT.Identity,
                                 bias=b[:, 2:3]).then_inc(x2_kept.sem, 1)

        def dve_bound(dve, n, i):
            dve.wait_ge(up_done.sem, up_done.count(n, 3))
            dve.wait_ge(weighted.sem, weighted.count(n - 1))
            nc.vector.tensor_scalar(x1[:].rearrange("p m v -> p (m v)"),
                                    x1_ps[:, 0:2 * UNIT].rearrange("p (t two) -> p t two", two=2)[:, :, 0],
                                    b[:, 1:2], None, ALU.add).then_inc(x1_kept.sem, 1)
            dve.wait_ge(x0_kept.sem, x0_kept.count(n))
            nc.vector.tensor_reduce(most[:], x0[i][:], axis=AX.X, op=ALU.max).then_inc(bound.sem, 1)
            nc.vector.tensor_reduce(least[:], x0[i][:], axis=AX.X, op=ALU.min).then_inc(bound.sem, 1)
            dve.wait_ge(bound.sem, bound.count(n, 2))
            dve.wait_ge(x1_kept.sem, x1_kept.count(n))
            for k, (x, y) in enumerate(((by_most, most), (by_least, least))):
                nc.vector.tensor_tensor(x[:], x1[:], y[:].unsqueeze(2).to_broadcast([P, 2, 2]), ALU.mult
                                        ).then_inc(bound.sem, 1)
            dve.wait_ge(bound.sem, bound.count(n, 4))
            nc.vector.tensor_tensor(by_most[:], by_most[:], by_least[:], ALU.max).then_inc(bound.sem, 1)
            dve.wait_ge(bound.sem, bound.count(n, 5))
            nc.vector.tensor_scalar(bias[:], by_most[:], -1.0, None, ALU.mult).then_inc(bound.sem, 1)

        def act_weigh(act, n, i, t):
            m, v = divmod(t, 2)
            if t == 0:
                act.wait_ge(bound.sem, bound.count(n))
                act.wait_ge(feats_done.sem, feats_done.count(n - 1))
            act.wait_ge(summed.sem, summed.count(n, t - 1))
            nc.scalar.activation(weight[t % 2][:], x0[i][:, m], ACT.Exp, scale=x1[:, m, v:v + 1],
                                 bias=bias[:, m, v:v + 1], accum_out=den[:, t:t + 1]).then_inc(weighted.sem, 1)

        def dve_sum(dve, n, i, t):
            dve.wait_ge(weighted.sem, weighted.count(n, t + 1))
            if t == 0:
                dve.wait_ge(x2_kept.sem, x2_kept.count(n))
            dve.wait_ge(summed.sem, summed.count(n, t - 1))
            nc.vector.tensor_tensor_reduce(out=product[t % 2][:], in0=weight[t % 2][:], in1=x2[i][:, t // 2], scale=1.0,
                                           scalar=0.0, op0=ALU.mult, op1=ALU.add, accum_out=num[:, t:t + 1]
                                           ).then_inc(summed.sem, 1)

        def dve_feats(dve, n):
            dve.wait_ge(summed.sem, summed.count(n))
            nc.vector.reciprocal(feats[:], den[:]).then_inc(feats_done.sem, 1)
            dve.wait_ge(feats_done.sem, feats_done.count(n, 1))
            nc.vector.tensor_tensor(feats[:], feats[:], num[:], ALU.mult).then_inc(feats_done.sem, 1)

        def act_sigmoid(act, n):
            act.wait_ge(feats_done.sem, feats_done.count(n))
            nc.scalar.activation(e_minus[:], feats[:], ACT.Exp, scale=-1.0).then_inc(e_done.sem, 1)

        def dve_gate(dve, n, i):
            dve.wait_ge(e_done.sem, e_done.count(n))
            nc.vector.tensor_scalar(gate[:], e_minus[:], 1.0, None, ALU.add).then_inc(gate_done.sem, 1)
            dve.wait_ge(gate_done.sem, gate_done.count(n, 1))
            nc.vector.reciprocal(gate[:], gate[:]).then_inc(gate_done.sem, 1)
            dve.wait_ge(gate_done.sem, gate_done.count(n, 2))
            for t in range(UNIT):
                x = columns(X, n, UNIT * C)[:, t * C:(t + 1) * C]
                nc.vector.scalar_tensor_tensor(out=x, in0=front.xn[i][:, t, 0], scalar=gate[:, t:t + 1], in1=x,
                                               op0=ALU.mult, op1=ALU.add).then_inc(x_added.sem, 1)

        def has(n):
            return not isinstance(n, int) or 0 <= n < UNITS

        def sp_step(sp, n, i):
            if has(n):
                moe.w_up.load(sp, ins, n, i)

        def pe_step(pe, n, i):
            if has(n):
                pe_up(pe, n, i)
            if has(n - 2):
                route.pe_rank(pe, n - 2, i)
            if has(n + 1):
                front.pe_transpose(pe, n + 1, 1 - i)
            if has(n - 1):
                route.front.pe_transpose(pe, n - 1, 1 - i)
                route.pe_logits(pe, n - 1, 1 - i)

        def act_step(act, n, i, q):
            if has(n):
                act_keep(act, n, i)
            if has(n - 2):
                route.act_gate(act, n - 2)
            if has(n + 1):
                front.act_norm(act, n + 1, 1 - i)
            if has(n - 1):
                route.front.act_norm(act, n - 1, 1 - i)
            if has(n):
                act_weigh(act, n, i, 0)
                act_weigh(act, n, i, 1)
            if has(n + 1):
                front.act_hi(act, n + 1, 1 - i)
            if has(n - 1):
                route.front.act_hi(act, n - 1, 1 - i)
            if has(n):
                act_weigh(act, n, i, 2)
                act_weigh(act, n, i, 3)
                moe.w_up.act_hi(act, n, i, q)
                act_sigmoid(act, n)

        def dve_step(dve, n, i, q):
            if has(n - 1):
                dve.wait_ge(x_added.sem, x_added.count(n - 1))
                route.front.dve_stats(dve, n - 1)
            if has(n + 2):
                front.dve_stats(dve, n + 2)
            if has(n - 2):
                route.dve_logits(dve, n - 2)
                route.dve_top(dve, n - 2)
            if has(n - 1):
                route.front.dve_mean_var(dve, n - 1)
            if has(n + 2):
                front.dve_mean_var(dve, n + 2)
            if has(n - 2):
                route.dve_choose(dve, n - 2, i)
            if has(n):
                dve_bound(dve, n, i)
            if has(n - 2):
                route.dve_room(dve, i, q - 1)
                route.dve_rows(dve, n - 2, i)
                route.dve_slots_gate(dve, n - 2, i)
            if has(n):
                dve_sum(dve, n, i, 0)
                dve_sum(dve, n, i, 1)
            if has(n + 1):
                front.dve_lo(dve, n + 1, 1 - i)
            if has(n - 1):
                route.front.dve_lo(dve, n - 1, 1 - i)
            if has(n):
                dve_sum(dve, n, i, 2)
                dve_sum(dve, n, i, 3)
                dve_feats(dve, n)
                moe.w_up.dve_lo(dve, n, i)
                dve_gate(dve, n, i)

        def pool_step(pool, n, i):
            if has(n - 1):
                route.front.pool_rstd(pool, n - 1)
            if has(n + 2):
                front.pool_rstd(pool, n + 2)
            if has(n - 2):
                route.pool_send(pool, n - 2, i)

        route.prepare()
        FIRST, LAST = 5, UNITS - 3
        with nc.Block() as block:
            @block.sync
            def _(sp):
                for n in range(FIRST):
                    sp_step(sp, n, n % 2)
                with nc.sync.Fori(FIRST // 2, LAST // 2) as k:
                    sp_step(sp, 2 * k + 1, 1)
                    sp_step(sp, 2 * k + 2, 0)
                for n in range(LAST, UNITS + 2):
                    sp_step(sp, n, n % 2)

            @block.tensor
            def _(pe):
                front.pe_transpose(pe, 0, 0)
                for n in range(FIRST):
                    pe_step(pe, n, n % 2)
                with nc.tensor.Fori(FIRST // 2, LAST // 2) as k:
                    pe_step(pe, 2 * k + 1, 1)
                    pe_step(pe, 2 * k + 2, 0)
                for n in range(LAST, UNITS + 2):
                    pe_step(pe, n, n % 2)

            @block.scalar
            def _(act):
                front.act_norm(act, 0, 0)
                front.act_hi(act, 0, 0)
                for n in range(FIRST):
                    act_step(act, n, n % 2, n // 2)
                with nc.scalar.Fori(FIRST // 2, LAST // 2) as k:
                    act_step(act, 2 * k + 1, 1, k)
                    act_step(act, 2 * k + 2, 0, k + 1)
                for n in range(LAST, UNITS + 2):
                    act_step(act, n, n % 2, n // 2)

            @block.vector
            def _(dve):
                for n in range(2):
                    front.dve_stats(dve, n)
                    front.dve_mean_var(dve, n)
                front.dve_lo(dve, 0, 0)
                for n in range(FIRST):
                    dve_step(dve, n, n % 2, n // 2)
                with nc.vector.Fori(FIRST // 2, LAST // 2) as k:
                    dve_step(dve, 2 * k + 1, 1, k)
                    dve_step(dve, 2 * k + 2, 0, k + 1)
                for n in range(LAST, UNITS + 2):
                    dve_step(dve, n, n % 2, n // 2)

            @block.gpsimd
            def _(pool):
                front.pool_rstd(pool, 0)
                front.pool_rstd(pool, 1)
                for n in range(FIRST):
                    pool_step(pool, n, n % 2)
                with nc.gpsimd.Fori(FIRST // 2, LAST // 2) as k:
                    pool_step(pool, 2 * k + 1, 1)
                    pool_step(pool, 2 * k + 2, 0)
                for n in range(LAST, UNITS + 2):
                    pool_step(pool, n, n % 2)
        clear(nc, used + front.used)


def build(nc, ins, out):
    with ExitStack() as ctx:
        X = ctx.enter_context(nc.sbuf_tensor("X", [P, TILES * C], F32))
        mem = {"ident": ctx.enter_context(nc.sbuf_tensor("ident_sb", [P, P], F32))}
        for name in ("minus_half", "minus_one", "eps6", "eps5"):
            mem[name] = ctx.enter_context(nc.sbuf_tensor(name, [P, UNIT], F32))
        stored = ctx.enter_context(nc.semaphore("stored"))
        mem["sent"] = [Signal(ctx, nc, f"sent{i}", 16 * 2 * UNIT) for i in range(2)]
        mem["filled"] = Signal(ctx, nc, "filled", 16)
        mem["y_sent"] = [Signal(ctx, nc, f"y_sent{i}", 16) for i in range(PASS)]
        with ExitStack() as first:
            moe0 = Moe(first, nc, "m0_", experts=16, chunks=1, hidden=128, guard=0.0)
            attention_phase(nc, mem, ins, X, moe0)
            experts_phase(nc, mem, X, moe0)
        moe1 = Moe(ctx, nc, "m1_", experts=8, chunks=6, hidden=114, guard=1e-9)
        mixing_phase(nc, mem, ins, X, moe1)
        experts_phase(nc, mem, X, moe1, out, stored)



def to_windows(x, np):
    x = np.roll(x, (-4, -4), axis=(1, 2))
    x = x.reshape(IMAGES, 2, 8, 2, 8, C).transpose(1, 2, 4, 0, 3, 5)
    return np.ascontiguousarray(x.reshape(P, IMAGES * 2 * C))


def from_windows(y, np):
    y = y.reshape(2, 8, 8, IMAGES, 2, C).transpose(3, 0, 1, 4, 2, 5).reshape(IMAGES, 16, 16, C)
    return np.ascontiguousarray(np.roll(y, (4, 4), axis=(1, 2)))


def lay_out(v, np):
    a = {}
    a["x"] = to_windows(v["x"], np)
    w_q, w_k, w_v = (v["L0_conv_w_qkv"][:, i * INNER:(i + 1) * INNER] for i in range(3))
    a["b_out2"] = np.tile(v["L0_conv_b_out"], (P, 2))
    a["wq_t"] = w_q.reshape(C, HEADS, HEAD_DIM).transpose(2, 1, 0).reshape(HEAD_DIM, HEADS * C)
    k_t = w_k.reshape(C, HEADS, HEAD_DIM).transpose(2, 1, 0)
    a["wk_t2"] = np.tile(k_t, (1, 1, 2)).reshape(HEAD_DIM, HEADS * 2 * C)
    blk = np.zeros((2, C, 2, INNER), w_v.dtype)
    blk[0, :, 0] = w_v
    blk[1, :, 1] = w_v
    a["wv_blk"] = blk.reshape(P, 2 * INNER)
    a["w_out"] = v["L0_conv_w_out"].reshape(2, P, C).transpose(1, 0, 2)
    t = np.arange(WIN)
    row, col = t // 8, t % 8
    rel = v["L0_conv_pos_emb"][row[None] - row[:, None] + 7, col[None] - col[:, None] + 7]
    a["rel_bias"] = np.tile(rel, (2, 1))
    lr = np.where((col[:, None] >= 4) != (col[None] >= 4), -3e38, 0.0).astype(np.float32)
    ul = np.where((row[:, None] >= 4) != (row[None] >= 4), -3e38, 0.0).astype(np.float32)
    a["mask"] = np.concatenate([np.stack([0 * ul, ul], 1), np.stack([lr, lr], 1)], 0)
    a["ident"] = np.eye(P, dtype=np.float32)
    up = np.stack([v["L0_ffn_w1"], v["L0_ffn_w2"]], 0)
    a["m0_w_up"] = np.tile(up.transpose(2, 1, 0, 3).reshape(C, -1), (2, 1))
    a["m0_w_down"] = v["L0_ffn_w3"].transpose(1, 0, 2).reshape(P, 16 * C)
    a["m0_router"] = np.tile(v["L0_ffn_gate_w"], (2, 1))
    a["m0_router_bias"] = np.tile(v["L0_ffn_gate_b"], (P, 1))
    a["m0_number"] = np.tile(np.arange(16, dtype=np.float32), (P, 1))
    cols = [np.tile(v[f"L1_conv_w{k}"][:, None], (2, w)) for k, w in ((1, P), (3, P), (2, 2))]
    a["mx_w"] = np.concatenate(cols, 1)
    a["mx_b"] = np.tile(np.concatenate([v["L1_conv_b1"], v["L1_conv_b2"], v["L1_conv_b3"]]), (P, 1))
    pad = np.zeros((2, 8, 684, C), np.float32)
    pad[0, :, :682], pad[1, :, :682] = v["L1_ffn_w1"], v["L1_ffn_w3"]
    a["m1_w_up"] = np.tile(pad.transpose(3, 1, 0, 2).reshape(C, -1), (2, 1))
    pad = np.zeros((8, C, 684), np.float32)
    pad[:, :, :682] = v["L1_ffn_w2"]
    a["m1_w_down"] = pad.reshape(8, C, 6, 114).transpose(3, 0, 2, 1).reshape(114, 48 * C)
    a["m1_router"] = np.tile(v["L1_ffn_router_w"].T, (2, 1))
    a["m1_router_bias"] = np.zeros((P, 8), np.float32)
    a["m1_number"] = np.tile(np.arange(8, dtype=np.float32), (P, 1))
    for prefix, experts in (("m0_", 16), ("m1_", 8)):
        a[prefix + "region_row"] = np.tile(P * (TILES + 1) * np.arange(experts, dtype=np.float32), (P, 1))
        a[prefix + "list_number"] = np.arange(2 * TILES + experts, dtype=np.float32)[None]
        fill = np.zeros((2 * experts * P, C + 2), np.float32)
        fill[:, C] = 2 * P * TILES + np.arange(2 * experts * P)
        a[prefix + "fill"] = fill
    a["before"] = np.triu(np.ones((P, P), np.float32), 1)
    a["threshold"] = np.tile(P * np.arange(TILES, dtype=np.float32), (P, 1))
    p, t, k = np.ogrid[0:P, 0:TILES, 0:2]
    a["done_row"] = ((k * P + p) * TILES + t).astype(np.float32).reshape(P, 2 * TILES)
    return {k: np.ascontiguousarray(x) for k, x in a.items()}


def kernel(**inputs):
    import numpy as np
    import concourse.bacc as bacc
    from concourse.bass_utils import run_bass_kernel_spmd

    arrays = lay_out({k: np.asarray(v) for k, v in inputs.items()}, np)
    nc = bacc.Bacc("TRN2", target_bir_lowering=False, num_devices=1)
    ins = {k: nc.dram_tensor("in_" + k, a.shape, F32, kind="ExternalInput").ap() for k, a in arrays.items()}
    out = nc.dram_tensor("out", (P, TILES * C), F32, kind="ExternalOutput").ap()
    build(nc, ins, out)
    r = run_bass_kernel_spmd(nc, [{"in_" + k: a for k, a in arrays.items()}], core_ids=[0])
    return from_windows(r.results[0]["out"], np)
```
